# Optimizing a Trainium2 kernel written in Bass

```python
import numpy as np
import jax
import jax.numpy as jnp

def _softmax(x, axis=-1):
    return jax.nn.softmax(x, axis=axis)

def _gelu(x):
    return jax.nn.gelu(x, approximate=True)

def _silu(x):
    return jax.nn.silu(x)

def _sigmoid(x):
    return jax.nn.sigmoid(x)

def _layernorm(x, axis=-1, eps=1e-05):
    m = jnp.mean(x, axis=axis, keepdims=True)
    v = jnp.var(x, axis=axis, keepdims=True)
    return (x - m) / jnp.sqrt(v + eps)

def _scatter_add(tgt, idx, src, axis=0):
    return tgt.at[idx].add(src)

def _segment_sum(src, seg, n):
    return jax.ops.segment_sum(src, seg, n)
kernel_name = 'mk_adj_resnorm_d4_adj_r2_e7beaf'

def setup_inputs(seed: int=0):
    np.random.seed(seed)
    _w = jnp.asarray

    def _rec_inputs():
        import jax
        import jax.numpy as jnp
        _gk = jax.random.key(seed)
        x = -0.0005207 + 1.001 * jax.random.normal(jax.random.fold_in(_gk, 1), (64, 128, 128), jnp.float32)
        _a = jax.random.bernoulli(jax.random.fold_in(_gk, 2), 0.015625, (64, 128, 128))
        _a = jnp.logical_or(_a, jnp.swapaxes(_a, -1, -2))
        _a = jnp.logical_or(_a, jnp.eye(128, dtype=bool))
        _af = _a.astype(jnp.float32)
        adj = _af
        _nm = jnp.ones((64, 128), dtype=bool)
        nodemask = _nm
        return (x, adj, nodemask)
    x, adj, nodemask = _rec_inputs()

    def _L0_gnn_setup():
        import jax, jax.numpy as jnp
        import numpy as np
        B, N, F, H = (16, 512, 128, 128)
        key = jax.random.key(seed)
        k1, k2, k3, k4, k5 = jax.random.split(key, 5)
        x = jax.random.normal(k1, (B, N, F), dtype=jnp.float32)
        adjacency = (jax.random.uniform(k2, (B, N, N)) < 0.05).astype(jnp.float32)
        node_mask = jax.random.uniform(k3, (B, N)) < 0.9
        W1 = jax.random.normal(k4, (F, H), dtype=jnp.float32) / np.sqrt(F)
        b1 = jnp.zeros((H,), dtype=jnp.float32)
        W2 = jax.random.normal(k5, (H, F), dtype=jnp.float32) / np.sqrt(H)
        b2 = jnp.zeros((F,), dtype=jnp.float32)
        eps = jnp.zeros((1,), dtype=jnp.float32)
        return {'x': x, 'adjacency': adjacency, 'node_mask': node_mask, 'W1': W1, 'b1': b1, 'W2': W2, 'b2': b2, 'eps': eps}
    _L0_gnn_all = _L0_gnn_setup()
    _L0_gnn_in = {k: v for k, v in _L0_gnn_all.items() if k in ('W1', 'b1', 'W2', 'b2', 'eps')}
    del _L0_gnn_all

    def _L1_gnn_setup():
        import jax, jax.numpy as jnp
        import numpy as np
        key = jax.random.key(seed)
        k1, k2, k3, k4 = jax.random.split(key, 4)
        B, N, D = (8, 1024, 128)
        embeddings = jax.random.normal(k1, (B, N, D), dtype=jnp.float32)
        adjacency_matrix = jax.random.uniform(k2, (B, N, N), dtype=jnp.float32)
        cost_matrix = jax.random.uniform(k3, (B, N, N), dtype=jnp.float32)
        W = jax.random.normal(k4, (D, 2 * D), dtype=jnp.float32) * (1.0 / np.sqrt(2 * D))
        b = jnp.zeros((D,), dtype=jnp.float32)
        return {'embeddings': embeddings, 'adjacency_matrix': adjacency_matrix, 'cost_matrix': cost_matrix, 'W': W, 'b': b}
    _L1_gnn_all = _L1_gnn_setup()
    _L1_gnn_in = {k: v for k, v in _L1_gnn_all.items() if k in ('W', 'b')}
    del _L1_gnn_all

    def _L2_gnn_setup():
        import jax, jax.numpy as jnp
        import numpy as np

        def _normalize_adjacency(adj):
            N = adj.shape[-1]
            adj_self = adj + jnp.eye(N, dtype=adj.dtype)
            rowsum = adj_self.sum(axis=2)
            d_inv_sqrt = rowsum ** (-0.5)
            d_inv_sqrt = jnp.where(jnp.isinf(d_inv_sqrt), 0.0, d_inv_sqrt)
            return adj_self * d_inv_sqrt[:, :, None] * d_inv_sqrt[:, None, :]
        key = jax.random.key(seed)
        k1, k2, k3 = jax.random.split(key, 3)
        B, N, Fin, Fout = (32, 512, 128, 128)
        x = jax.random.normal(k1, (B, N, Fin), dtype=jnp.float32)
        adj = jax.random.uniform(k2, (B, N, N), dtype=jnp.float32)
        limit = float(np.sqrt(6.0 / (Fin + Fout)))
        weight = jax.random.uniform(k3, (Fin, Fout), dtype=jnp.float32, minval=-limit, maxval=limit)
        bias = jnp.zeros((Fout,), dtype=jnp.float32)
        return {'x': x, 'adj': adj, 'weight': weight, 'bias': bias}
    _L2_gnn_all = _L2_gnn_setup()
    _L2_gnn_in = {k: v for k, v in _L2_gnn_all.items() if k in ('weight', 'bias')}
    del _L2_gnn_all

    def _L3_gnn_setup():
        import jax, jax.numpy as jnp
        import numpy as np
        B, S, H, HID = (1, 512, 128, 128)
        LN_EPS = 1e-05

        def _layernorm(y, gamma, beta):
            mu = jnp.mean(y, axis=-1, keepdims=True)
            var = jnp.mean(jnp.square(y - mu), axis=-1, keepdims=True)
            return (y - mu) * jax.lax.rsqrt(var + LN_EPS) * gamma + beta
        key = jax.random.key(seed)
        ks = jax.random.split(key, 8)
        x = jax.random.normal(ks[0], (B, S, H), dtype=jnp.float32)
        adj = jax.random.uniform(ks[1], (B, S, S), dtype=jnp.float32)
        W1 = jax.random.normal(ks[2], (2 * H, HID), dtype=jnp.float32) / np.sqrt(2 * H)
        b1 = jnp.zeros((HID,), dtype=jnp.float32)
        W2 = jax.random.normal(ks[3], (HID, HID), dtype=jnp.float32) / np.sqrt(HID)
        b2 = jnp.zeros((HID,), dtype=jnp.float32)
        gamma = jnp.ones((HID,), dtype=jnp.float32)
        beta = jnp.zeros((HID,), dtype=jnp.float32)
        return {'x': x, 'adj': adj, 'W1': W1, 'b1': b1, 'W2': W2, 'b2': b2, 'gamma': gamma, 'beta': beta}
    _L3_gnn_all = _L3_gnn_setup()
    _L3_gnn_in = {k: v for k, v in _L3_gnn_all.items() if k in ('W1', 'b1', 'W2', 'b2', 'gamma', 'beta')}
    del _L3_gnn_all
    return {'x': x, 'adj': adj, 'nodemask': nodemask, 'L0_gnn_W1': _L0_gnn_in['W1'], 'L0_gnn_b1': _L0_gnn_in['b1'], 'L0_gnn_W2': _L0_gnn_in['W2'], 'L0_gnn_b2': _L0_gnn_in['b2'], 'L0_gnn_eps': _L0_gnn_in['eps'], 'L1_gnn_W': _L1_gnn_in['W'], 'L1_gnn_b': _L1_gnn_in['b'], 'L2_gnn_weight': _L2_gnn_in['weight'], 'L2_gnn_bias': _L2_gnn_in['bias'], 'L3_gnn_W1': _L3_gnn_in['W1'], 'L3_gnn_b1': _L3_gnn_in['b1'], 'L3_gnn_W2': _L3_gnn_in['W2'], 'L3_gnn_b2': _L3_gnn_in['b2'], 'L3_gnn_gamma': _L3_gnn_in['gamma'], 'L3_gnn_beta': _L3_gnn_in['beta']}

def reference(x, adj, nodemask, L0_gnn_W1, L0_gnn_b1, L0_gnn_W2, L0_gnn_b2, L0_gnn_eps, L1_gnn_W, L1_gnn_b, L2_gnn_weight, L2_gnn_bias, L3_gnn_W1, L3_gnn_b1, L3_gnn_W2, L3_gnn_b2, L3_gnn_gamma, L3_gnn_beta):
    import jax
    import jax.numpy as jnp

    def _L0_gnn_ref(x, adjacency, node_mask, W1, b1, W2, b2, eps):
        import jax, jax.numpy as jnp
        import numpy as np
        B, N, F, H = (16, 512, 128, 128)
        x_agg = jnp.einsum('bnf,bnm->bmf', x, adjacency)
        h = (1.0 + eps) * x + x_agg
        y = jnp.maximum(h @ W1 + b1, 0.0) @ W2 + b2
        return jnp.where(node_mask[..., None], y, jnp.zeros((), dtype=y.dtype))

    def _L1_gnn_ref(embeddings, adjacency_matrix, cost_matrix, W, b):
        import jax, jax.numpy as jnp
        import numpy as np
        degree = adjacency_matrix.sum(axis=-1)[:, :, None]
        sum_neighbors = jnp.einsum('bid,bij->bjd', embeddings, cost_matrix) / degree
        concatenated = jnp.concatenate([embeddings, sum_neighbors], axis=-1)
        out = jnp.einsum('bnk,dk->bnd', concatenated, W) + b
        return jax.nn.relu(out)

    def _L2_gnn_ref(x, adj, weight, bias):
        import jax, jax.numpy as jnp
        import numpy as np

        def _normalize_adjacency(adj):
            N = adj.shape[-1]
            adj_self = adj + jnp.eye(N, dtype=adj.dtype)
            rowsum = adj_self.sum(axis=2)
            d_inv_sqrt = rowsum ** (-0.5)
            d_inv_sqrt = jnp.where(jnp.isinf(d_inv_sqrt), 0.0, d_inv_sqrt)
            return adj_self * d_inv_sqrt[:, :, None] * d_inv_sqrt[:, None, :]
        adj_norm = _normalize_adjacency(adj)
        support = jnp.einsum('bni,io->bno', x, weight)
        out = jnp.einsum('bnm,bmo->bno', adj_norm, support) + bias
        return out

    def _L3_gnn_ref(x, adj, W1, b1, W2, b2, gamma, beta):
        import jax, jax.numpy as jnp
        import numpy as np
        B, S, H, HID = (1, 512, 128, 128)
        LN_EPS = 1e-05

        def _layernorm(y, gamma, beta):
            mu = jnp.mean(y, axis=-1, keepdims=True)
            var = jnp.mean(jnp.square(y - mu), axis=-1, keepdims=True)
            return (y - mu) * jax.lax.rsqrt(var + LN_EPS) * gamma + beta
        hi = jnp.einsum('bsh,hk->bsk', x, W1[:H])
        hj = jnp.einsum('bsh,hk->bsk', x, W1[H:])
        h = jax.nn.relu(hi[:, :, None, :] + hj[:, None, :, :] + b1)
        y = jnp.einsum('bijk,kl->bijl', h, W2) + b2
        y = _layernorm(y, gamma, beta)
        out = jnp.einsum('bij,bijh->bih', adj, y)
        return out
    x = _layernorm(x + _L0_gnn_ref(x, adj, nodemask, L0_gnn_W1, L0_gnn_b1, L0_gnn_W2, L0_gnn_b2, L0_gnn_eps), axis=-1)
    x = _layernorm(x + _L1_gnn_ref(x, adj, adj, L1_gnn_W, L1_gnn_b), axis=-1)
    x = _layernorm(x + _L2_gnn_ref(x, adj, L2_gnn_weight, L2_gnn_bias), axis=-1)
    x = _layernorm(x + _L3_gnn_ref(x, adj, L3_gnn_W1, L3_gnn_b1, L3_gnn_W2, L3_gnn_b2, L3_gnn_gamma, L3_gnn_beta), axis=-1)
    return x

_drawn_inputs = setup_inputs


def setup_inputs(seed=0):
    import zlib

    import numpy as np

    out = dict(_drawn_inputs(seed))
    spreads = {'L0_gnn_b1': (0.0, 0.1),
     'L0_gnn_b2': (0.0, 0.1),
     'L1_gnn_b': (0.0, 0.1),
     'L2_gnn_bias': (0.0, 0.1),
     'L3_gnn_b1': (0.0, 0.1),
     'L3_gnn_b2': (0.0, 0.1),
     'L3_gnn_gamma': (1.0, 0.2),
     'L3_gnn_beta': (0.0, 0.1)}
    factors = {}
    for name, (base, spread) in spreads.items():
        noise = np.random.default_rng([zlib.crc32(name.encode()), seed]).standard_normal(out[name].shape)
        drawn = base * np.exp(spread * noise) if base else spread * noise
        out[name] = jnp.asarray(drawn.astype(out[name].dtype))
    for name, factor in factors.items():
        out[name] = (out[name] * factor).astype(out[name].dtype)
    return out
```

```python
import concourse.bass as bass
from concourse import mybir
from contextlib import ExitStack

P = 128
B = 64
GROUP = 4
GROUPS = B // GROUP
GW = GROUP * P
CH = 384
TILES = CH // P
FAST_CHUNKS = 2
CAPACITY = FAST_CHUNKS * CH
ALL_CHUNKS = -(-P * P // CH)
LN_EPS = 1e-5

MATS = ["L0_W1", "L0_W2", "L1_WaT", "L1_WbT", "L2_W", "L3_W1a", "L3_W1b", "L3_W2"]
ROWS = ["L0_b2", "L1_b", "L2_b", "L3_b1", "L3_b2", "gamma", "beta"]
COLS = ["L0_b1", "L0_eps"]
CONST_W = (len(MATS) + len(ROWS)) * P + len(COLS)


def gnn_stack(nc, x_d, a_d, at_d, mask_d, const_d, a_g, at_g, out_d):
    f32, bf16, f16 = mybir.dt.float32, mybir.dt.bfloat16, mybir.dt.float16
    i32, u8 = mybir.dt.int32, mybir.dt.uint8
    ALU = mybir.AluOpType
    ACT = mybir.ActivationFunctionType
    AX = mybir.AxisListType

    hi_s = nc.dram_tensor("hi_scratch", (B, P, P), f32).ap()
    hj_s = nc.dram_tensor("hj_scratch", (B, P, P), f32).ap()
    res_s = nc.dram_tensor("res_scratch", (B, P, P), f32).ap()

    ctx = ExitStack()
    with ctx:
        def sb(name, shape, dt=f32):
            return ctx.enter_context(nc.sbuf_tensor(name, shape, dt))

        def sem(name):
            return ctx.enter_context(nc.semaphore(name))

        const = sb("const", [P, CONST_W])
        C = {n: const[:, i * P:(i + 1) * P] for i, n in enumerate(MATS + ROWS)}
        at = (len(MATS) + len(ROWS)) * P
        for i, n in enumerate(COLS):
            C[n] = const[:, at + i:at + i + 1]
        ident = sb("ident", [P, P])
        tri = sb("tri", [P, P], bf16)
        ones_b = sb("ones_b", [P, P], bf16)
        zeros = sb("zeros", [P, P])
        edge_i = sb("edge_i", [P, CAPACITY], i32)
        edge = sb("edge", [P, CAPACITY])
        edge1 = sb("edge1", [P, CAPACITY])
        scaled_id = sb("scaled_id", [P, P])
        eps_col = sb("eps_col", [P, 1])
        mask8 = sb("mask8", [P, B], u8)
        mask = sb("mask", [P, B])
        seeds = sb("seeds", [P, 4])
        w2mean = sb("w2mean", [P, 1])
        w2c = sb("w2c", [P, P])
        b2mean = sb("b2mean", [P, 1])
        b2c = sb("b2c", [P, P])
        split = [sb(f"split{n}", [P, P]) for n in range(4)]
        part = [sb(f"part{n}", [P, P], bf16) for n in range(6)]
        bias0 = sb("bias0", [P, GROUP, P], bf16)
        bias3 = sb("bias3", [P, TILES, P], bf16)

        K2 = range(2)
        X = [sb(f"X{k}", [P, GROUP, P]) for k in K2]
        A = [sb(f"A{k}", [P, GROUP, P]) for k in K2]
        AT = [sb(f"AT{k}", [P, GROUP, P]) for k in K2]
        A0 = [sb(f"A0{k}", [P, GROUP, P]) for k in K2]
        tmpT = [sb(f"tmpT{k}", [P, GROUP, P]) for k in K2]
        rT = [sb(f"rT{k}", [P, GROUP, P]) for k in K2]
        R = [sb(f"R{k}", [P, GROUP, P]) for k in K2]
        pb = [sb(f"pb{k}", [P, GROUP, P]) for k in K2]
        z = [sb(f"z{k}", [P, GROUP, P]) for k in K2]
        t = [sb(f"t{k}", [P, GROUP, P]) for k in K2]
        xn = [[sb(f"xn{l}{k}", [P, GROUP, P]) for k in K2] for l in range(3)]
        ssb = [sb(f"ssb{k}", [P, GROUP, P]) for k in K2]
        xb = [sb(f"xb{k}", [P, GROUP, P]) for k in K2]
        xb0 = [sb(f"xb0{k}", [P, GROUP, P]) for k in K2]
        sdis = [sb(f"sdis{k}", [P, GROUP, P]) for k in K2]
        bdeg = [sb(f"bdeg{k}", [P, GROUP, P]) for k in K2]
        res = [sb(f"res{k}", [P, GROUP, P]) for k in K2]
        hi = [sb(f"hi{k}", [P, GROUP, P]) for k in K2]
        hj = [sb(f"hj{k}", [P, GROUP, P]) for k in K2]
        isedge = [sb(f"isedge{k}", [P, GROUP, P], bf16) for k in K2]
        stats = [sb(f"stats{k}", [P, GROUP, 6]) for k in K2]
        mv = [sb(f"mv{k}", [P, GROUP, 2]) for k in K2]
        std = [sb(f"std{k}", [P, GROUP]) for k in K2]
        rstd = [sb(f"rstd{k}", [P, GROUP]) for k in K2]
        deg = [sb(f"deg{k}", [P, GROUP]) for k in K2]
        rdeg = [sb(f"rdeg{k}", [P, GROUP]) for k in K2]
        rs0 = [sb(f"rs0{k}", [P, GROUP]) for k in K2]
        rsafe = [sb(f"rsafe{k}", [P, GROUP]) for k in K2]
        rsq = [sb(f"rsq{k}", [P, GROUP]) for k in K2]
        dis0 = [sb(f"dis0{k}", [P, GROUP]) for k in K2]
        dis = [sb(f"dis{k}", [P, GROUP]) for k in K2]
        maskg = [sb(f"maskg{k}", [P, GROUP]) for k in K2]

        cnt = sb("cnt", [P, B], bf16)
        cntf = sb("cntf", [P, B])
        end = sb("end", [P, B])
        off = sb("off", [P, B])
        most = sb("most", [1, 1])
        most_i = sb("most_i", [1, 1], i32)

        gA = [sb(f"gA{q}", [P, P]) for q in K2]
        gAT = [sb(f"gAT{q}", [P, P]) for q in K2]
        gHI = [sb(f"gHI{q}", [P, P]) for q in K2]
        gHJ = [sb(f"gHJ{q}", [P, P]) for q in K2]
        gRES = [sb(f"gRES{q}", [P, P]) for q in K2]
        nz = [sb(f"nz{q}", [P, P]) for q in K2]
        rank = [sb(f"rank{q}", [P, P]) for q in K2]
        pos = [sb(f"pos{q}", [P, P], f16) for q in K2]
        pos32 = sb("pos32", [P, P])
        below = sb("below", [P, CAPACITY])
        S = [sb(f"S{q}", [P, CAPACITY]) for q in K2]
        T = [sb(f"T{c}", [P, CH]) for c in K2]
        hT = [sb(f"hT{c}", [P, CH]) for c in K2]
        ST = [sb(f"ST{c}", [P, TILES, P]) for c in K2]
        sq = sb("sq", [P, TILES, P])
        ysb = [sb(f"ysb{c}", [P, TILES, P]) for c in K2]
        WS = [sb(f"WS{c}", [P, TILES, P]) for c in K2]
        ssum = sb("ssum", [P, TILES])
        esd = sb("esd", [P, TILES])
        erstd = sb("erstd", [P, TILES])
        gout = [sb(f"gout{q}", [P, P]) for q in K2]
        tout = [sb(f"tout{q}", [P, P]) for q in K2]
        ostats = [sb(f"ostats{q}", [P, 6]) for q in K2]
        omv = [sb(f"omv{q}", [P, 2]) for q in K2]
        ostd = [sb(f"ostd{q}", [P, 1]) for q in K2]
        orstd = [sb(f"orstd{q}", [P, 1]) for q in K2]
        y4 = [sb(f"y4{q}", [P, P]) for q in K2]
        acc = sb("acc", [P, P])
        goff = sb("goff", [P, 1])
        gend = sb("gend", [P, 1])
        invp = 1.0 / P

        bank = [ctx.enter_context(nc.psum_tensor(f"bank{n}", [P, 512], f32)) for n in range(8)]

        def psA(k, n):
            return bank[4 * k + n][:, :].rearrange("p (g f) -> p g f", g=GROUP)

        def flat(ap):
            return ap[:, :, :].rearrange("p g f -> p (g f)")

        V_ps = bank[0][:, 0:CH]
        H_ps = bank[1][:, 0:CH]
        ST_ps = bank[2][:, 0:CH].rearrange("p (t f) -> p t f", t=TILES)
        M_ps = [bank[3 + c][:, 0:CH].rearrange("p (t f) -> p t f", t=TILES) for c in K2]
        Y_ps = [bank[5 + c][:, 0:CH].rearrange("p (t f) -> p t f", t=TILES) for c in K2]
        O_ps = bank[7][:, 0:P]

        s_const = sem("const_loaded")
        s_mask = sem("mask_loaded")
        s_setp = sem("pool_setup_done")
        s_v = sem("vector_setup_steps")
        s_setv = sem("vector_setup_done")

        x_loaded = [sem(f"x_loaded{k}") for k in K2]
        a_loaded = [sem(f"a_loaded{k}") for k in K2]
        at_loaded = [sem(f"at_loaded{k}") for k in K2]
        names = ["a0_ready", "deg_done", "rs0_done", "rsafe_ready", "rsq_ready", "dis0_done", "dis_ready",
                 "hT_psum", "hT_ready", "u_psum", "rT_ready", "y_psum", "mask_ready",
                 "t0_done", "stats0", "var0", "std0", "rstd0", "x1_ready",
                 "x1T_psum", "x1T_ready", "pR_psum", "R_ready", "pb_done", "q_psum", "z_done",
                 "t1_done", "stats1", "var1", "std1", "rstd1", "x2_ready",
                 "x2T_psum", "x2T_ready", "s_psum", "s_ready", "o_psum", "xb0_done", "sdis_done", "xb_ready",
                 "t2_done", "stats2", "var2", "std2", "rstd2", "x3_ready",
                 "x3T_psum", "x3T_ready", "hh_psum", "hi_ready", "hj_ready",
                 "isedge_done", "edges_counted", "bdeg_done", "res_ready"]
        s = {n: sem(n) for n in names}
        stored = [sem(f"group_stored{k}") for k in K2]

        cnt_ready = sem("cnt_ready")
        count_psum = sem("count_psum")
        most_done = sem("most_done")
        end_ready = sem("end_ready")
        most_ready = sem("most_ready")

        ga_loaded = [sem(f"ga_loaded{q}") for q in K2]
        gh_loaded = [sem(f"gh_loaded{q}") for q in K2]
        gres_loaded = [sem(f"gres_loaded{q}") for q in K2]
        b = {n: sem("e_" + n) for n in
             ["nz_done", "rank_done", "pos_ready", "below_done", "S_ready", "V_psum", "T_ready",
              "H_psum", "hT_ready", "M_psum", "ST_ready", "Y_psum", "sq_ready", "y_ready",
              "ssum_ready", "sd_ready", "rstd_done", "WS_ready", "O_psum",
              "gamma_done", "t_done", "stats_done", "var_ready", "ostd_ready", "orstd_done", "out_ready",
              "shifted", "acc_done"]}
        out_stored = [sem(f"out_stored{q}") for q in K2]
    
        SLOT_STORED = GROUPS // 2 * 3 * 16 + 1

        block = ctx.enter_context(nc.Block())

        @block.sync
        def _(sp):
            sp.dma_start(const[:, :], const_d).then_inc(s_const, 16)
            sp.dma_start(mask8[:, :], mask_d).then_inc(s_mask, 16)

            def load(dst, src, group, sm):
                sp.dma_start(flat(dst), src[bass.ds(group, 1), :, :].rearrange("o p c -> p (o c)")).then_inc(sm, 16)

            for k in K2:
                load(A[k], a_d, k, a_loaded[k])
                load(X[k], x_d, k, x_loaded[k])
                load(AT[k], at_d, k, at_loaded[k])

            def group_step(it, more):
                for k in K2:
                    n = 2 * it + k + 1
                    if more:
                        sp.wait_ge(s["t0_done"], n)
                        load(X[k], x_d, 2 * it + 2 + k, x_loaded[k])
                for k in K2:
                    n = 2 * it + k + 1
                    if more:
                        sp.wait_ge(s["z_done"], n)
                        sp.wait_ge(s["isedge_done"], n)
                        load(A[k], a_d, 2 * it + 2 + k, a_loaded[k])
                for k in K2:
                    n = 2 * it + k + 1
                    if more:
                        sp.wait_ge(s["t2_done"], n)
                        load(AT[k], at_d, 2 * it + 2 + k, at_loaded[k])
                for k in K2:
                    n = 2 * it + k + 1
                    for buf, dst, ready in ((res, res_s, "res_ready"), (hi, hi_s, "hi_ready"), (hj, hj_s, "hj_ready")):
                        sp.wait_ge(s[ready], n)
                        sp.dma_start(dst[bass.ds(4 * (2 * it + k), GROUP), :, :].rearrange("g p f -> p g f"),
                                     buf[k][:, :, :]).then_inc(stored[k], 16)

            with sp.Fori(0, GROUPS // 2 - 1) as it:
                group_step(it, True)
            group_step(GROUPS // 2 - 1, False)
            for k in K2:
                sp.wait_ge(stored[k], SLOT_STORED)

            def load_a(g, q):
                sp.dma_start(gA[q][:, :], a_g[bass.ds(g, 1), :, :].rearrange("o p c -> p (o c)")).then_inc(ga_loaded[q], 16)

            def load_h(g, q):
                for dst, src in ((gHI, hi_s), (gHJ, hj_s), (gAT, at_g)):
                    sp.dma_start(dst[q][:, :], src[bass.ds(g, 1), :, :].rearrange("o p c -> p (o c)")).then_inc(gh_loaded[q], 16)

            def load_res(g, q):
                sp.dma_start(gRES[q][:, :], res_s[bass.ds(g, 1), :, :].rearrange("o p c -> p (o c)")).then_inc(gres_loaded[q], 16)

            def store(g, q, n):
                sp.wait_ge(b["out_ready"], n)
                sp.dma_start(out_d[bass.ds(g, 1), :, :].rearrange("o p c -> p (o c)"), y4[q][:, :]).then_inc(out_stored[q], 16)

            sp.wait_ge(most_ready, 1)
            fullest = sp.value_load(most_i[0:1, 0:1], min_val=0, max_val=P * P)
            with sp.If(fullest > CAPACITY):
                with sp.Fori(0, B) as g:
                    load_a(g, 0)
                    load_h(g, 0)
                    load_res(g, 0)
                    store(g, 0, g + 1)
                sp.wait_ge(out_stored[0], 16 * B + 1)
            with sp.Else():
                for q in K2:
                    load_a(q, q)
                    load_h(q, q)
                    load_res(q, q)

                def pair_step(p, first, more):
                    for q in K2:
                        g = 2 * p + q
                        if more:
                            sp.wait_ge(b["pos_ready"], g + 1)
                            load_a(g + 2, q)
                    for q in K2:
                        g = 2 * p + q
                        if more:
                            sp.wait_ge(b["M_psum"], 2 * g + 2)
                            load_h(g + 2, q)
                        if not (first and q == 0):
                            if not (first and q == 1):
                                store(g - 2, q, g - 1)
                    for q in K2:
                        g = 2 * p + q
                        if more:
                            sp.wait_ge(b["t_done"], g + 1)
                            load_res(g + 2, q)

                pair_step(0, True, True)
                with sp.Fori(1, B // 2 - 1) as p:
                    pair_step(p, False, True)
                pair_step(B // 2 - 1, False, False)
                store(B - 2, 0, B - 1)
                store(B - 1, 1, B)
                for q in K2:
                    sp.wait_ge(out_stored[q], 8 * B + 1)

        @block.gpsimd
        def _(pool):
            nc.gpsimd.memset(zeros[:, :], 0.0)
            nc.gpsimd.memset(ident[:, :], 0.0)
            nc.gpsimd.memset(ones_b[:, :], 1.0)
            nc.gpsimd.memset(tri[:, :], 1.0)
            nc.gpsimd.memset(eps_col[:, :], LN_EPS)
            nc.gpsimd.memset(bias0[:, :, :], 0.0)
            nc.gpsimd.memset(bias3[:, :, :], 0.0)
            nc.gpsimd.iota(edge_i[:, :], pattern=[[1, CAPACITY]], base=0, channel_multiplier=0).then_inc(s_setp, 1)
            pool.wait_ge(s_setp, 1)
            nc.gpsimd.affine_select(out=ident[:, :], in_=ident[:, :], compare_op=ALU.not_equal, fill=1.0,
                                    base=0, pattern=[[-1, P]], channel_multiplier=1)
            nc.gpsimd.affine_select(out=tri[:, :], in_=tri[:, :], compare_op=ALU.is_ge, fill=0.0,
                                    base=0, pattern=[[1, P]], channel_multiplier=-1).then_inc(s_setp, 1)
            pool.wait_ge(s_setv, 1)
            beta = C["beta"]
            with pool.Fori(0, GROUPS // 2) as it:
                for k in K2:
                    n = 2 * it + k + 1
                    nc.gpsimd.tensor_copy(maskg[k][:, :], mask[:, bass.ds(4 * (2 * it + k), GROUP)]).then_inc(s["mask_ready"], 1)
                for k in K2:
                    n = 2 * it + k + 1
                    pool.wait_ge(s["deg_done"], n)
                    nc.gpsimd.tensor_tensor(bdeg[k][:, :, :], beta.unsqueeze(1).to_broadcast([P, GROUP, P]),
                                            deg[k][:, :].unsqueeze(2).to_broadcast([P, GROUP, P]), ALU.mult).then_inc(s["bdeg_done"], 1)
                for k in K2:
                    n = 2 * it + k + 1
                    pool.wait_ge(s["x2_ready"], n)
                    nc.gpsimd.tensor_tensor(xb0[k][:, :, :], xn[1][k][:, :, :],
                                            C["L2_b"].unsqueeze(1).to_broadcast([P, GROUP, P]), ALU.add).then_inc(s["xb0_done"], 1)
                for k in K2:
                    n = 2 * it + k + 1
                    pool.wait_ge(s["s_ready"], n)
                    nc.gpsimd.tensor_tensor(sdis[k][:, :, :], ssb[k][:, :, :],
                                            dis[k][:, :].unsqueeze(2).to_broadcast([P, GROUP, P]), ALU.mult).then_inc(s["sdis_done"], 1)
                    pool.wait_ge(s["sdis_done"], n)
                    pool.wait_ge(s["xb0_done"], n)
                    nc.gpsimd.tensor_tensor(xb[k][:, :, :], xb0[k][:, :, :], sdis[k][:, :, :], ALU.add).then_inc(s["xb_ready"], 1)
                for k in K2:
                    n = 2 * it + k + 1
                    pool.wait_ge(s["x3_ready"], n)
                    pool.wait_ge(s["bdeg_done"], n)
                    pool.wait_ge(stored[k], 48 * it + 1)
                    nc.gpsimd.tensor_tensor(res[k][:, :, :], xn[2][k][:, :, :], bdeg[k][:, :, :], ALU.add).then_inc(s["res_ready"], 1)
                pool.wait_ge(s["res_ready"], 2 * it + 2)

        @block.scalar
        def _(act):
            act.wait_ge(s_const, 16)
            act.wait_ge(s_setp, 2)

            def ln_std(k, n, layer):
                act.wait_ge(s[f"var{layer}"], n)
                nc.scalar.activation(std[k][:, :], mv[k][:, :, 1], ACT.Sqrt, bias=eps_col[:, 0:1]).then_inc(s[f"std{layer}"], 1)

            def evict(k, n, ps, dst, wait, done, func=ACT.Copy, **kw):
                act.wait_ge(s[wait], n)
                nc.scalar.activation(dst[k][:, :, :], ps, func, **kw).then_inc(s[done], 1)

            with act.Fori(0, GROUPS // 2) as it:
                ns = [2 * it + 1, 2 * it + 2]
                for k, n in enumerate(ns):
                    evict(k, n, psA(k, 0), tmpT, "hT_psum", "hT_ready")
                for k, n in enumerate(ns):
                    act.wait_ge(s["rsafe_ready"], n)
                    nc.scalar.activation(rsq[k][:, :], rsafe[k][:, :], ACT.Sqrt).then_inc(s["rsq_ready"], 1)
                for k, n in enumerate(ns):
                    evict(k, n, psA(k, 1), rT, "u_psum", "rT_ready", ACT.Relu, bias=C["L0_b1"])
                for k, n in enumerate(ns):
                    ln_std(k, n, 0)
                for k, n in enumerate(ns):
                    evict(k, n, psA(k, 1), tmpT, "x1T_psum", "x1T_ready")
                for k, n in enumerate(ns):
                    evict(k, n, psA(k, 3), R, "pR_psum", "R_ready")
                for k, n in enumerate(ns):
                    ln_std(k, n, 1)
                for k, n in enumerate(ns):
                    evict(k, n, psA(k, 1), tmpT, "x2T_psum", "x2T_ready")
                for k, n in enumerate(ns):
                    ln_std(k, n, 2)
                for k, n in enumerate(ns):
                    evict(k, n, psA(k, 1), tmpT, "x3T_psum", "x3T_ready")
                for k, n in enumerate(ns):
                    act.wait_ge(stored[k], 48 * it + 1)
                    evict(k, n, psA(k, 3), hj, "hh_psum", "hj_ready")

            def relu(c, n):
                act.wait_ge(b["H_psum"], n)
                nc.scalar.activation(hT[c][:, :], H_ps, ACT.Relu).then_inc(b["hT_ready"], 1)

            def starts(c, n):
                act.wait_ge(b["M_psum"], n)
                nc.scalar.activation(ST[c][:, :, :], ST_ps, ACT.Copy).then_inc(b["ST_ready"], 1)

            def spread(n):
                act.wait_ge(b["ssum_ready"], n)
                nc.scalar.activation(esd[:, :], ssum[:, :], ACT.Sqrt, bias=eps_col[:, 0:1], scale=invp).then_inc(b["sd_ready"], 1)

            def square(c, n):
                act.wait_ge(b["Y_psum"], n)
                nc.scalar.activation(sq[:, :, :], Y_ps[c], ACT.Square).then_inc(b["sq_ready"], 1)
                nc.scalar.activation(ysb[c][:, :, :], Y_ps[c], ACT.Copy).then_inc(b["y_ready"], 1)

            def out_std(q, n):
                act.wait_ge(b["var_ready"], n)
                nc.scalar.activation(ostd[q][:, :], omv[q][:, 1:2], ACT.Sqrt, bias=eps_col[:, 0:1]).then_inc(b["ostd_ready"], 1)

            act.wait_ge(most_ready, 1)
            fullest = act.value_load(most_i[0:1, 0:1], min_val=0, max_val=P * P)
            with act.If(fullest > CAPACITY):
                with act.Fori(0, B) as g:
                    with act.Fori(0, ALL_CHUNKS) as c:
                        n = g * ALL_CHUNKS + c + 1
                        relu(0, n)
                        starts(0, n)
                        square(0, n)
                        spread(n)
                    out_std(0, g + 1)
            with act.Else():
                def pair_step(p, first):
                    for q in K2:
                        g = 2 * p + q
                        for c in K2:
                            n = 2 * g + c + 1
                            relu(c, n)
                            starts(c, n)
                            if not (first and q == 0 and c == 0):
                                spread(n - 1)
                            square(c, n)
                            if c == 1 and not (first and q == 0):
                                out_std(1 - q, g)

                pair_step(0, True)
                with act.Fori(1, B // 2) as p:
                    pair_step(p, False)
                spread(2 * B)
                out_std(1, B)

        @block.vector
        def _(dve):
            step = [0]

            def then(ins):
                ins.then_inc(s_v, 1)
                step[0] += 1
                dve.wait_ge(s_v, step[0])

            dve.wait_ge(s_setp, 2)
            dve.wait_ge(s_const, 16)
            dve.wait_ge(s_mask, 16)
            nc.vector.tensor_copy(mask[:, :], mask8[:, :])
            nc.vector.tensor_copy(edge[:, :], edge_i[:, :])
            then(nc.vector.tensor_scalar(w2mean[:, :], C["L0_eps"], 1.0, None, ALU.add))
            then(nc.vector.tensor_scalar(scaled_id[:, :], ident[:, :], w2mean[:, 0:1], None, ALU.mult))
            nc.vector.tensor_scalar(edge1[:, :], edge[:, :], 1.0, None, ALU.add)
            nc.vector.tensor_reduce(b2mean[:, :], C["L3_b2"], AX.X, ALU.add)
            then(nc.vector.tensor_reduce(w2mean[:, :], C["L3_W2"], AX.X, ALU.add))
            nc.vector.tensor_scalar(b2mean[:, :], b2mean[:, :], invp, None, ALU.mult)
            then(nc.vector.tensor_scalar(w2mean[:, :], w2mean[:, :], invp, None, ALU.mult))
            nc.vector.tensor_scalar(b2c[:, :], C["L3_b2"], b2mean[:, 0:1], None, ALU.subtract)
            then(nc.vector.tensor_scalar(w2c[:, :], C["L3_W2"], w2mean[:, 0:1], None, ALU.subtract))
            for row, bias, copies, m in ((C["L0_b2"], bias0, GROUP, 0), (b2c[:, :], bias3, TILES, 3)):
                then(nc.vector.tensor_copy(part[m][:, :], row))
                then(nc.vector.tensor_tensor(split[0][:, :], row, part[m][:, :], ALU.subtract))
                then(nc.vector.tensor_copy(part[m + 1][:, :], split[0][:, :]))
                then(nc.vector.tensor_tensor(split[1][:, :], split[0][:, :], part[m + 1][:, :], ALU.subtract))
                then(nc.vector.tensor_copy(part[m + 2][:, :], split[1][:, :]))
                for r in range(3):
                    for c in range(copies):
                        last = nc.vector.tensor_copy(bias[32 * r:32 * r + 1, c, :], part[m + r][32 * r:32 * r + 1, :])
                then(last)
            for i, counter in enumerate(stored + out_stored):
                nc.vector.memset(seeds[:, i:i + 1], 0.0).then_inc(counter, 1)
            nc.vector.memset(ssum[:, :], 0.0).then_inc(s_setv, 1)

            def ln_stats(k, n, layer):
                dve.wait_ge(s[f"t{layer}_done"], n)
                for g in range(GROUP):
                    last = nc.vector.bn_stats(stats[k][:, g, :], t[k][:, g, :])
                last.then_inc(s[f"stats{layer}"], 1)

            def ln_var(k, n, layer):
                dve.wait_ge(s_const, 16)
                dve.wait_ge(s[f"stats{layer}"], n)
                for g in range(GROUP):
                    last = nc.vector.bn_aggr(mv[k][:, g, :], stats[k][:, g, :])
                last.then_inc(s[f"var{layer}"], 1)

            def ln_rstd(k, n, layer):
                dve.wait_ge(s[f"std{layer}"], n)
                nc.vector.reciprocal(rstd[k][:, :], std[k][:, :]).then_inc(s[f"rstd{layer}"], 1)

            def ln_apply(k, n, layer):
                dve.wait_ge(s[f"rstd{layer}"], n)
                for g in range(GROUP):
                    last = nc.vector.tensor_scalar(xn[layer][k][:, g, :], t[k][:, g, :], mv[k][:, g, 0:1],
                                                   rstd[k][:, g:g + 1], ALU.subtract, ALU.mult)
                last.then_inc(s[f"x{layer + 1}_ready"], 1)

            def layer_norm(ns, layer):
                for stage in (ln_stats, ln_var, ln_rstd, ln_apply):
                    for k, n in enumerate(ns):
                        stage(k, n, layer)

            with dve.Fori(0, GROUPS // 2) as it:
                ns = [2 * it + 1, 2 * it + 2]
                for k, n in enumerate(ns):
                    dve.wait_ge(a_loaded[k], 16 * it + 16)
                    nc.vector.tensor_tensor(A0[k][:, :, :], A[k][:, :, :],
                                            scaled_id[:, :].unsqueeze(1).to_broadcast([P, GROUP, P]), ALU.add).then_inc(s["a0_ready"], 1)
                for k, n in enumerate(ns):
                    nc.vector.tensor_reduce(deg[k][:, :], A[k][:, :, :], AX.X, ALU.add).then_inc(s["deg_done"], 1)
                for k, n in enumerate(ns):
                    dve.wait_ge(s["deg_done"], n)
                    nc.vector.reciprocal(rdeg[k][:, :], deg[k][:, :])
                    nc.vector.tensor_scalar(rs0[k][:, :], deg[k][:, :], 1.0, 0.0, ALU.add, ALU.is_equal).then_inc(s["rs0_done"], 1)
                for k, n in enumerate(ns):
                    dve.wait_ge(s["rs0_done"], n)
                    nc.vector.scalar_tensor_tensor(rsafe[k][:, :], deg[k][:, :], 1.0, rs0[k][:, :], ALU.add, ALU.add).then_inc(s["rsafe_ready"], 1)
                for k, n in enumerate(ns):
                    dve.wait_ge(s["rsq_ready"], n)
                    nc.vector.reciprocal(dis0[k][:, :], rsq[k][:, :]).then_inc(s["dis0_done"], 1)
                for k, n in enumerate(ns):
                    dve.wait_ge(s["dis0_done"], n)
                    nc.vector.scalar_tensor_tensor(dis[k][:, :], rs0[k][:, :], 0.0, dis0[k][:, :], ALU.is_equal, ALU.mult).then_inc(s["dis_ready"], 1)
                for k, n in enumerate(ns):
                    dve.wait_ge(s["mask_ready"], n)
                    dve.wait_ge(x_loaded[k], 16 * it + 16)
                    dve.wait_ge(s["y_psum"], n)
                    for g in range(GROUP):
                        last = nc.vector.scalar_tensor_tensor(t[k][:, g, :], psA(k, 0)[:, g, :], maskg[k][:, g:g + 1],
                                                              X[k][:, g, :], ALU.mult, ALU.add)
                    last.then_inc(s["t0_done"], 1)
                layer_norm(ns, 0)
                for k, n in enumerate(ns):
                    nc.vector.tensor_scalar(isedge[k][:, :, :], A[k][:, :, :], 0.0, None, ALU.not_equal).then_inc(s["isedge_done"], 1)
                for k, n in enumerate(ns):
                    dve.wait_ge(s["isedge_done"], n)
                    nc.vector.tensor_reduce(cntf[:, bass.ds(4 * (2 * it + k), GROUP)], isedge[k][:, :, :], AX.X, ALU.add).then_inc(s["edges_counted"], 1)
                for k, n in enumerate(ns):
                    dve.wait_ge(s["pR_psum"], n)
                    nc.vector.tensor_tensor(pb[k][:, :, :], psA(k, 2), C["L1_b"].unsqueeze(1).to_broadcast([P, GROUP, P]), ALU.add).then_inc(s["pb_done"], 1)
                for k, n in enumerate(ns):
                    dve.wait_ge(s["q_psum"], n)
                    dve.wait_ge(s["pb_done"], n)
                    for g in range(GROUP):
                        last = nc.vector.scalar_tensor_tensor(z[k][:, g, :], psA(k, 0)[:, g, :], rdeg[k][:, g:g + 1],
                                                              pb[k][:, g, :], ALU.mult, ALU.add)
                    last.then_inc(s["z_done"], 1)
                for k, n in enumerate(ns):
                    dve.wait_ge(s["z_done"], n)
                    nc.vector.scalar_tensor_tensor(flat(t[k]), flat(z[k]), 0.0, flat(xn[0][k]), ALU.max, ALU.add).then_inc(s["t1_done"], 1)
                layer_norm(ns, 1)
                for k, n in enumerate(ns):
                    dve.wait_ge(s["s_psum"], n)
                    dve.wait_ge(s["dis_ready"], n)
                    nc.vector.tensor_tensor(ssb[k][:, :, :], psA(k, 2), dis[k][:, :].unsqueeze(2).to_broadcast([P, GROUP, P]), ALU.mult).then_inc(s["s_ready"], 1)
                for k, n in enumerate(ns):
                    dve.wait_ge(s["o_psum"], n)
                    dve.wait_ge(s["xb_ready"], n)
                    for g in range(GROUP):
                        last = nc.vector.scalar_tensor_tensor(t[k][:, g, :], psA(k, 0)[:, g, :], dis[k][:, g:g + 1],
                                                              xb[k][:, g, :], ALU.mult, ALU.add)
                    last.then_inc(s["t2_done"], 1)
                layer_norm(ns, 2)
                for k, n in enumerate(ns):
                    dve.wait_ge(s["hh_psum"], n)
                    dve.wait_ge(stored[k], 48 * it + 1)
                    nc.vector.tensor_tensor(hi[k][:, :, :], psA(k, 2), C["L3_b1"].unsqueeze(1).to_broadcast([P, GROUP, P]), ALU.add).then_inc(s["hi_ready"], 1)

            dve.wait_ge(s["edges_counted"], GROUPS)
            nc.vector.tensor_copy(cnt[:, :], cntf[:, :]).then_inc(cnt_ready, 1)
            dve.wait_ge(count_psum, 1)
            nc.vector.tensor_copy(end[:, :], bank[0][:, 0:B]).then_inc(end_ready, 1)
            nc.vector.tensor_reduce(most[0:1, :], bank[1][0:1, 0:B], AX.X, ALU.max).then_inc(most_done, 1)
            dve.wait_ge(end_ready, 1)
            nc.vector.tensor_tensor(off[:, :], end[:, :], cntf[:, :], ALU.subtract).then_inc(end_ready, 1)
            dve.wait_ge(most_done, 1)
            nc.vector.tensor_copy(most_i[0:1, :], most[0:1, :]).then_inc(most_ready, 1)

            def prep_rank(q, g):
                nc.vector.tensor_scalar(nz[q][:, :], gA[q][:, :], 0.0, None, ALU.not_equal).then_inc(b["nz_done"], 1)
                dve.wait_ge(b["nz_done"], g + 1)
                nc.vector.tensor_tensor_scan(rank[q][:, :], nz[q][:, :], zeros[:, :], 0.0, ALU.add, ALU.add).then_inc(b["rank_done"], 1)
                dve.wait_ge(b["rank_done"], g + 1)

            def prep(q, g, load):
                dve.wait_ge(ga_loaded[q], load)
                nc.vector.tensor_scalar(below[:, :], edge[:, :], end[:, bass.ds(g, 1)], None, ALU.is_lt).then_inc(b["below_done"], 1)
                prep_rank(q, g)
                nc.vector.scalar_tensor_tensor(pos[q][:, :], rank[q][:, :], off[:, bass.ds(g, 1)], nz[q][:, :],
                                               ALU.add, ALU.mult).then_inc(b["pos_ready"], 1)
                dve.wait_ge(b["below_done"], g + 1)
                nc.vector.scalar_tensor_tensor(S[q][:, :], edge[:, :], off[:, bass.ds(g, 1)], below[:, :],
                                               ALU.is_ge, ALU.mult).then_inc(b["S_ready"], 1)

            def ends(c, e0, n):
                dve.wait_ge(b["V_psum"], n)
                nc.vector.tensor_tensor(T[c][:, :], V_ps, edge1[:, e0:e0 + CH], ALU.is_equal).then_inc(b["T_ready"], 1)

            def weigh(c, n):
                dve.wait_ge(b["sq_ready"], n)
                nc.vector.tensor_reduce(ssum[:, :], sq[:, :, :], AX.X, ALU.add).then_inc(b["ssum_ready"], 1)
                dve.wait_ge(b["sd_ready"], n)
                nc.vector.reciprocal(erstd[:, :], esd[:, :]).then_inc(b["rstd_done"], 1)
                dve.wait_ge(b["rstd_done"], n)
                dve.wait_ge(b["ST_ready"], n)
                for i in range(TILES):
                    last = nc.vector.scalar_tensor_tensor(WS[c][:, i, :], M_ps[c][:, i, :], erstd[:, i:i + 1],
                                                          ST[c][:, i, :], ALU.mult, ALU.mult)
                last.then_inc(b["WS_ready"], 1)

            def scale_sum(q, src):
                nc.vector.tensor_tensor(gout[q][:, :], src, C["gamma"], ALU.mult).then_inc(b["gamma_done"], 1)

            def norm_stats(q, g, load):
                dve.wait_ge(b["gamma_done"], g + 1)
                dve.wait_ge(gres_loaded[q], load)
                nc.vector.tensor_tensor(tout[q][:, :], gout[q][:, :], gRES[q][:, :], ALU.add).then_inc(b["t_done"], 1)
                dve.wait_ge(b["t_done"], g + 1)
                nc.vector.bn_stats(ostats[q][:, :], tout[q][:, :]).then_inc(b["stats_done"], 1)
                dve.wait_ge(s_const, 16)
                dve.wait_ge(b["stats_done"], g + 1)
                nc.vector.bn_aggr(omv[q][:, :], ostats[q][:, :]).then_inc(b["var_ready"], 1)

            def norm_apply(q, g, stores):
                dve.wait_ge(b["ostd_ready"], g + 1)
                nc.vector.reciprocal(orstd[q][:, :], ostd[q][:, :]).then_inc(b["orstd_done"], 1)
                dve.wait_ge(b["orstd_done"], g + 1)
                dve.wait_ge(out_stored[q], stores)
                nc.vector.tensor_scalar(y4[q][:, :], tout[q][:, :], omv[q][:, 0:1], orstd[q][:, 0:1],
                                        ALU.subtract, ALU.mult).then_inc(b["out_ready"], 1)

            dve.wait_ge(most_ready, 1)
            dve.wait_ge(end_ready, 2)
            fullest = dve.value_load(most_i[0:1, 0:1], min_val=0, max_val=P * P)
            with dve.If(fullest > CAPACITY):
                with dve.Fori(0, B) as g:
                    dve.wait_ge(ga_loaded[0], 16 * g + 16)
                    nc.vector.tensor_copy(goff[:, :], off[:, bass.ds(g, 1)])
                    nc.vector.tensor_copy(gend[:, :], end[:, bass.ds(g, 1)])
                    nc.vector.memset(acc[:, :], 0.0)
                    prep_rank(0, g)
                    nc.vector.scalar_tensor_tensor(pos32[:, :], rank[0][:, :], goff[:, 0:1], nz[0][:, :],
                                                   ALU.add, ALU.mult).then_inc(b["shifted"], 1)
                    with dve.Fori(0, ALL_CHUNKS) as c:
                        n = g * ALL_CHUNKS + c + 1
                        dve.wait_ge(b["shifted"], n + g)
                        nc.vector.tensor_copy(pos[0][:, :], pos32[:, :]).then_inc(b["pos_ready"], 1)
                        nc.vector.tensor_scalar(below[:, 0:CH], edge[:, 0:CH], gend[:, 0:1], None, ALU.is_lt).then_inc(b["below_done"], 1)
                        dve.wait_ge(b["below_done"], n)
                        nc.vector.scalar_tensor_tensor(S[0][:, 0:CH], edge[:, 0:CH], goff[:, 0:1], below[:, 0:CH],
                                                       ALU.is_ge, ALU.mult).then_inc(b["S_ready"], 1)
                        ends(0, 0, n)
                        weigh(0, n)
                        dve.wait_ge(b["S_ready"], n)
                        nc.vector.tensor_scalar(pos32[:, :], pos32[:, :], float(CH), None, ALU.subtract)
                        nc.vector.tensor_scalar(goff[:, :], goff[:, :], float(CH), None, ALU.subtract)
                        nc.vector.tensor_scalar(gend[:, :], gend[:, :], float(CH), None, ALU.subtract).then_inc(b["shifted"], 1)
                        dve.wait_ge(b["O_psum"], n)
                        nc.vector.tensor_tensor(acc[:, :], acc[:, :], O_ps, ALU.add).then_inc(b["acc_done"], 1)
                        dve.wait_ge(b["acc_done"], n)
                    scale_sum(0, acc[:, :])
                    norm_stats(0, g, 16 * g + 16)
                    norm_apply(0, g, 16 * g + 1)
            with dve.Else():
                def pair_step(p, first, more):
                    for q in K2:
                        g = 2 * p + q
                        for c in K2:
                            n = 2 * g + c + 1
                            ends(c, c * CH, n)
                            if c == 1 and not (first and q == 0):
                                dve.wait_ge(b["O_psum"], g)
                                scale_sum(1 - q, O_ps)
                            if not (first and q == 0 and c == 0):
                                weigh(1 - c, n - 1)
                            if c == 0:
                                if q == 0:
                                    prep(1, g + 1, 16 * p + 16)
                                elif more:
                                    prep(0, g + 1, 16 * p + 32)
                                if not first:
                                    norm_apply(q, g - 2, 16 * (p - 1) + 1)
                            elif not (first and q == 0):
                                norm_stats(1 - q, g - 1, 16 * (p + q))

                prep(0, 0, 16)
                pair_step(0, True, True)
                with dve.Fori(1, B // 2 - 1) as p:
                    pair_step(p, False, True)
                pair_step(B // 2 - 1, False, False)
                weigh(1, 2 * B)
                norm_apply(0, B - 2, 8 * B - 15)
                dve.wait_ge(b["O_psum"], B)
                scale_sum(1, O_ps)
                norm_stats(1, B - 1, 8 * B)
                norm_apply(1, B - 1, 8 * B - 15)

        @block.tensor
        def _(pe):
            pe.wait_ge(s_setv, 1)
            pe.wait_ge(s_setp, 2)

            def products(k, bk, lhs, rhs, done, bias=None):
                if bias is not None:
                    nc.tensor.matmul(flat(psA(k, bk)), ones_b[:, :], flat(bias), start=True, stop=False)
                for g in range(GROUP):
                    last = nc.tensor.matmul(psA(k, bk)[:, g, :], lhs(g), rhs(g), start=bias is None,
                                            stop=bias is None or g == GROUP - 1)
                if done:
                    last.then_inc(s[done], 1)

            def transposes(k, src, done):
                for g in range(GROUP):
                    last = nc.tensor.transpose(psA(k, 1)[:, g, :], src[k][:, g, :], ident[:, :])
                last.then_inc(s[done], 1)

            with pe.Fori(0, GROUPS // 2) as it:
                ns = [2 * it + 1, 2 * it + 2]
                for k, n in enumerate(ns):
                    pe.wait_ge(s["a0_ready"], n)
                    pe.wait_ge(x_loaded[k], 16 * it + 16)
                    products(k, 0, lambda g: X[k][:, g, :], lambda g: A0[k][:, g, :], "hT_psum")
                for k, n in enumerate(ns):
                    pe.wait_ge(s["hT_ready"], n)
                    nc.tensor.matmul(flat(psA(k, 1)), C["L0_W1"], flat(tmpT[k]), start=True, stop=True).then_inc(s["u_psum"], 1)
                for k, n in enumerate(ns):
                    pe.wait_ge(s["rT_ready"], n)
                    products(k, 0, lambda g: rT[k][:, g, :], lambda g: C["L0_W2"], "y_psum", bias=bias0)
                for k, n in enumerate(ns):
                    pe.wait_ge(s["x1_ready"], n)
                    transposes(k, xn[0], "x1T_psum")
                for k, n in enumerate(ns):
                    pe.wait_ge(s["x1T_ready"], n)
                    products(k, 3, lambda g: tmpT[k][:, g, :], lambda g: C["L1_WbT"], None)
                    products(k, 2, lambda g: tmpT[k][:, g, :], lambda g: C["L1_WaT"], "pR_psum")
                for k, n in enumerate(ns):
                    pe.wait_ge(s["R_ready"], n)
                    products(k, 0, lambda g: A[k][:, g, :], lambda g: R[k][:, g, :], "q_psum")
                for k, n in enumerate(ns):
                    pe.wait_ge(s["x2_ready"], n)
                    transposes(k, xn[1], "x2T_psum")
                for k, n in enumerate(ns):
                    pe.wait_ge(s["x2T_ready"], n)
                    products(k, 2, lambda g: tmpT[k][:, g, :], lambda g: C["L2_W"], "s_psum")
                for k, n in enumerate(ns):
                    pe.wait_ge(s["s_ready"], n)
                    pe.wait_ge(at_loaded[k], 16 * it + 16)
                    products(k, 0, lambda g: AT[k][:, g, :], lambda g: ssb[k][:, g, :], "o_psum")
                for k, n in enumerate(ns):
                    pe.wait_ge(s["x3_ready"], n)
                    transposes(k, xn[2], "x3T_psum")
                for k, n in enumerate(ns):
                    pe.wait_ge(s["x3T_ready"], n)
                    products(k, 3, lambda g: tmpT[k][:, g, :], lambda g: C["L3_W1b"], None)
                    products(k, 2, lambda g: tmpT[k][:, g, :], lambda g: C["L3_W1a"], "hh_psum")

            pe.wait_ge(cnt_ready, 1)
            pe.wait_ge(s["hj_ready"], GROUPS)
            nc.tensor.matmul(bank[0][:, 0:B], tri[:, :], cnt[:, :], start=True, stop=True)
            nc.tensor.matmul(bank[1][:, 0:B], ones_b[:, :], cnt[:, :], start=True, stop=True).then_inc(count_psum, 1)

            def place(q, c, n_s):
                pe.wait_ge(b["S_ready"], n_s)
                nc.tensor.matmul(V_ps, pos[q][:, :], S_half(q, c), start=True, stop=True).then_inc(b["V_psum"], 1)

            def S_half(q, c):
                return S[q][:, c * CH:(c + 1) * CH].bitcast(bf16).rearrange("p (e h) -> p e h", h=2)[:, :, 1]

            def gather(q, c, slot, n, load):
                pe.wait_ge(b["T_ready"], n)
                pe.wait_ge(gh_loaded[q], load)
                nc.tensor.matmul(H_ps, gHI[q][:, :], S[q][:, c * CH:(c + 1) * CH], start=True, stop=False)
                nc.tensor.matmul(H_ps, gHJ[q][:, :], T[slot][:, :], start=False, stop=True).then_inc(b["H_psum"], 1)

            def rows(q, c, slot, n, first):
                if not first:
                    pe.wait_ge(b["ST_ready"], n - 1)
                for i in range(TILES):
                    nc.tensor.transpose(ST_ps[:, i, :], S[q][:, c * CH + i * P:c * CH + (i + 1) * P], ident[:, :])
                for i in range(TILES):
                    last = nc.tensor.matmul(M_ps[slot][:, i, :], T[slot][:, i * P:(i + 1) * P], gAT[q][:, :], start=True, stop=True)
                last.then_inc(b["M_psum"], 1)

            def mlp(slot, n):
                pe.wait_ge(b["hT_ready"], n)
                nc.tensor.matmul(Y_ps[slot].rearrange("p t f -> p (t f)"), ones_b[:, :], flat(bias3), start=True, stop=False)
                for i in range(TILES):
                    last = nc.tensor.matmul(Y_ps[slot][:, i, :], hT[slot][:, i * P:(i + 1) * P], w2c[:, :], start=False, stop=i == TILES - 1)
                last.then_inc(b["Y_psum"], 1)

            def scatter(q, slot, n, start, stop):
                pe.wait_ge(b["WS_ready"], n)
                pe.wait_ge(b["y_ready"], n)
                for i in range(TILES):
                    last = nc.tensor.matmul(O_ps, WS[slot][:, i, :], ysb[slot][:, i, :],
                                            start=start and i == 0, stop=stop and i == TILES - 1)
                if stop:
                    last.then_inc(b["O_psum"], 1)

            pe.wait_ge(most_ready, 1)
            fullest = pe.value_load(most_i[0:1, 0:1], min_val=0, max_val=P * P)
            with pe.If(fullest > CAPACITY):
                with pe.Fori(0, B) as g:
                    with pe.Fori(0, ALL_CHUNKS) as c:
                        n = g * ALL_CHUNKS + c + 1
                        place(0, 0, n)
                        gather(0, 0, 0, n, 48 * g + 48)
                        rows(0, 0, 0, n, True)
                        mlp(0, n)
                        scatter(0, 0, n, True, True)
            with pe.Else():
                def pair_step(p, first, last):
                    for q in K2:
                        g = 2 * p + q
                        for c in K2:
                            n = 2 * g + c + 1
                            gather(q, c, c, n, 48 * p + 48)
                            rows(q, c, c, n, first and q == 0 and c == 0)
                            if c == 0:
                                place(q, 1, g + 1)
                            elif not (last and q == 1):
                                place(1 - q, 0, g + 2)
                            mlp(c, n)
                            if not (first and q == 0 and c == 0):
                                scatter(q if c else 1 - q, 1 - c, n - 1, c == 1, c == 0)

                place(0, 0, 1)
                pair_step(0, True, False)
                with pe.Fori(1, B // 2 - 1) as p:
                    pair_step(p, False, False)
                pair_step(B // 2 - 1, False, True)
                scatter(1, 1, 2 * B, False, True)


def kernel(x, adj, nodemask, L0_gnn_W1, L0_gnn_b1, L0_gnn_W2, L0_gnn_b2, L0_gnn_eps, L1_gnn_W, L1_gnn_b,
           L2_gnn_weight, L2_gnn_bias, L3_gnn_W1, L3_gnn_b1, L3_gnn_W2, L3_gnn_b2, L3_gnn_gamma, L3_gnn_beta):
    import numpy as np
    import concourse.bacc as bacc
    from concourse.bass_utils import run_bass_kernel_spmd

    x, adj = np.asarray(x), np.asarray(adj)

    def grouped(a):
        return np.ascontiguousarray(a.reshape(GROUPS, GROUP, P, P).transpose(0, 2, 1, 3).reshape(GROUPS, P, GW))

    adj_t = np.ascontiguousarray(adj.transpose(0, 2, 1))
    w1 = np.asarray(L1_gnn_W)
    w3 = np.asarray(L3_gnn_W1)
    mats = [L0_gnn_W1, L0_gnn_W2, w1[:, :P].T, w1[:, P:].T, L2_gnn_weight, w3[:P], w3[P:], L3_gnn_W2]
    rows = [L0_gnn_b2, L1_gnn_b, L2_gnn_bias, L3_gnn_b1, L3_gnn_b2, L3_gnn_gamma, L3_gnn_beta]
    cols = [np.asarray(L0_gnn_b1).reshape(P, 1), np.broadcast_to(np.asarray(L0_gnn_eps).reshape(1, 1), (P, 1))]
    consts = np.ascontiguousarray(np.concatenate(
        [np.asarray(m) for m in mats] + [np.broadcast_to(np.asarray(r).reshape(1, P), (P, P)) for r in rows] + cols, axis=1))
    arrays = {
        "x_groups": grouped(x), "adj_groups": grouped(adj), "adjT_groups": grouped(adj_t),
        "nodemask_T": np.ascontiguousarray(np.asarray(nodemask).T).view(np.uint8), "constants": consts,
        "adj": np.ascontiguousarray(adj), "adj_T": adj_t,
    }
    nc = bacc.Bacc("TRN2", target_bir_lowering=False, num_devices=1)
    ap = {n: nc.dram_tensor(n, a.shape, mybir.dt.from_np(a.dtype), kind="ExternalInput").ap() for n, a in arrays.items()}
    out = nc.dram_tensor("out", (B, P, P), mybir.dt.float32, kind="ExternalOutput").ap()
    gnn_stack(nc, ap["x_groups"], ap["adj_groups"], ap["adjT_groups"], ap["nodemask_T"], ap["constants"],
              ap["adj"], ap["adj_T"], out)
    r = run_bass_kernel_spmd(nc, [arrays], core_ids=[0])
    return r.results[0]["out"]
```

```python
import concourse.bass as bass
from concourse import mybir
from contextlib import ExitStack

P = 128
B = 64
GROUP = 4
GROUPS = B // GROUP
GW = GROUP * P
CH = 384
TILES = CH // P
FAST_CHUNKS = 2
CAPACITY = FAST_CHUNKS * CH
ALL_CHUNKS = -(-P * P // CH)
LN_EPS = 1e-5

MATS = ["L0_W1", "L0_W2", "L1_WaT", "L1_WbT", "L2_W", "L3_W1a", "L3_W1b", "L3_W2"]
ROWS = ["L0_b2", "L1_b", "L2_b", "L3_b1", "L3_b2", "gamma", "beta"]
COLS = ["L0_b1", "L0_eps"]
CONST_W = (len(MATS) + len(ROWS)) * P + len(COLS)


def gnn_stack(nc, x_d, a_d, at_d, mask_d, const_d, a_g, at_g, out_d):
    f32, bf16, f16 = mybir.dt.float32, mybir.dt.bfloat16, mybir.dt.float16
    i32, u8 = mybir.dt.int32, mybir.dt.uint8
    f32r = mybir.dt.float32r
    ALU = mybir.AluOpType
    ACT = mybir.ActivationFunctionType
    AX = mybir.AxisListType

    hi_s = nc.dram_tensor("hi_scratch", (B, P, P), f32).ap()
    hj_s = nc.dram_tensor("hj_scratch", (B, P, P), f32).ap()
    res_s = nc.dram_tensor("res_scratch", (B, P, P), f32).ap()

    ctx = ExitStack()
    with ctx:
        def sb(name, shape, dt=f32):
            return ctx.enter_context(nc.sbuf_tensor(name, shape, dt))

        def sem(name):
            return ctx.enter_context(nc.semaphore(name))

        const = sb("const", [P, CONST_W])
        C = {n: const[:, i * P:(i + 1) * P] for i, n in enumerate(MATS + ROWS)}
        at = (len(MATS) + len(ROWS)) * P
        for i, n in enumerate(COLS):
            C[n] = const[:, at + i:at + i + 1]
        ident = sb("ident", [P, P])
        tri = sb("tri", [P, P], bf16)
        ones_b = sb("ones_b", [P, P], bf16)
        zeros = sb("zeros", [P, P])
        edge_i = sb("edge_i", [P, CAPACITY], i32)
        edge = sb("edge", [P, CAPACITY])
        edge1 = sb("edge1", [P, CAPACITY])
        scaled_id = sb("scaled_id", [P, P])
        eps_col = sb("eps_col", [P, 1])
        mask8 = sb("mask8", [P, B], u8)
        mask = sb("mask", [P, B])
        seeds = sb("seeds", [P, 4])
        w2mean = sb("w2mean", [P, 1])
        w2c = sb("w2c", [P, P])
        b2mean = sb("b2mean", [P, 1])
        b2c = sb("b2c", [P, P])
        split = [sb(f"split{n}", [P, P]) for n in range(4)]
        part = [sb(f"part{n}", [P, P], bf16) for n in range(6)]
        bias0 = sb("bias0", [P, GROUP, P], bf16)
        bias3 = sb("bias3", [P, TILES, P], bf16)

        K2 = range(2)
        X = [sb(f"X{k}", [P, GROUP, P]) for k in K2]
        A = [sb(f"A{k}", [P, GROUP, P]) for k in K2]
        AT = [sb(f"AT{k}", [P, GROUP, P]) for k in K2]
        A0 = [sb(f"A0{k}", [P, GROUP, P]) for k in K2]
        tmpT = [sb(f"tmpT{k}", [P, GROUP, P]) for k in K2]
        rT = [sb(f"rT{k}", [P, GROUP, P]) for k in K2]
        R = [sb(f"R{k}", [P, GROUP, P]) for k in K2]
        pb = [sb(f"pb{k}", [P, GROUP, P]) for k in K2]
        z = [sb(f"z{k}", [P, GROUP, P]) for k in K2]
        t = [sb(f"t{k}", [P, GROUP, P]) for k in K2]
        xn = [[sb(f"xn{l}{k}", [P, GROUP, P]) for k in K2] for l in range(3)]
        ssb = [sb(f"ssb{k}", [P, GROUP, P]) for k in K2]
        xb = [sb(f"xb{k}", [P, GROUP, P]) for k in K2]
        xb0 = [sb(f"xb0{k}", [P, GROUP, P]) for k in K2]
        sdis = [sb(f"sdis{k}", [P, GROUP, P]) for k in K2]
        bdeg = [sb(f"bdeg{k}", [P, GROUP, P]) for k in K2]
        res = [sb(f"res{k}", [P, GROUP, P]) for k in K2]
        hi = [sb(f"hi{k}", [P, GROUP, P]) for k in K2]
        hj = [sb(f"hj{k}", [P, GROUP, P]) for k in K2]
        isedge = [sb(f"isedge{k}", [P, GROUP, P], bf16) for k in K2]
        stats = [sb(f"stats{k}", [P, GROUP, 6]) for k in K2]
        mv = [sb(f"mv{k}", [P, GROUP, 2]) for k in K2]
        std = [sb(f"std{k}", [P, GROUP]) for k in K2]
        rstd = [sb(f"rstd{k}", [P, GROUP]) for k in K2]
        deg = [sb(f"deg{k}", [P, GROUP]) for k in K2]
        rdeg = [sb(f"rdeg{k}", [P, GROUP]) for k in K2]
        rs0 = [sb(f"rs0{k}", [P, GROUP]) for k in K2]
        rsafe = [sb(f"rsafe{k}", [P, GROUP]) for k in K2]
        rsq = [sb(f"rsq{k}", [P, GROUP]) for k in K2]
        dis0 = [sb(f"dis0{k}", [P, GROUP]) for k in K2]
        dis = [sb(f"dis{k}", [P, GROUP]) for k in K2]
        maskg = [sb(f"maskg{k}", [P, GROUP]) for k in K2]

        cnt = sb("cnt", [P, B], bf16)
        cntf = sb("cntf", [P, B])
        end = sb("end", [P, B])
        off = sb("off", [P, B])
        most = sb("most", [1, 1])
        most_i = sb("most_i", [1, 1], i32)

        gA = [sb(f"gA{q}", [P, P]) for q in K2]
        gH = [sb(f"gH{q}", [P, 3, P]) for q in K2]
        gHu = [sb(f"gHu{q}", [P, 3, P], f32r) for q in K2]
        gHl = [sb(f"gHl{q}", [P, 3, P], f32r) for q in K2]
        gRES = [sb(f"gRES{q}", [P, P]) for q in K2]
        nz = [sb(f"nz{q}", [P, P]) for q in K2]
        rank = [sb(f"rank{q}", [P, P]) for q in K2]
        pos = [sb(f"pos{q}", [P, P], f32r) for q in K2]
        pos32 = sb("pos32", [P, P])
        below = [sb(f"below{q}", [P, CAPACITY]) for q in K2]
        S = [sb(f"S{q}", [P, CAPACITY], f32r) for q in K2]
        T = [sb(f"T{c}", [P, CH], f32r) for c in K2]
        hT = [sb(f"hT{c}", [P, CH]) for c in K2]
        ST = [sb(f"ST{c}", [P, TILES, P]) for c in K2]
        sq = [sb(f"sq{c}", [P, TILES, P]) for c in K2]
        ysb = [sb(f"ysb{c}", [P, TILES, P]) for c in K2]
        WS = [sb(f"WS{c}", [P, TILES, P]) for c in K2]
        ssum = sb("ssum", [P, TILES])
        esd = sb("esd", [P, TILES])
        erstd = sb("erstd", [P, TILES])
        gout = [sb(f"gout{q}", [P, P]) for q in K2]
        tout = [sb(f"tout{q}", [P, P]) for q in K2]
        ostats = [sb(f"ostats{q}", [P, 6]) for q in K2]
        omv = [sb(f"omv{q}", [P, 2]) for q in K2]
        ostd = [sb(f"ostd{q}", [P, 1]) for q in K2]
        orstd = [sb(f"orstd{q}", [P, 1]) for q in K2]
        y4 = [sb(f"y4{q}", [P, P]) for q in K2]
        acc = sb("acc", [P, P])
        goff = sb("goff", [P, 1])
        gend = sb("gend", [P, 1])
        invp = 1.0 / P

        bank = [ctx.enter_context(nc.psum_tensor(f"bank{n}", [P, 512], f32)) for n in range(8)]

        def psA(k, n):
            return bank[4 * k + n][:, :].rearrange("p (g f) -> p g f", g=GROUP)

        def flat(ap):
            return ap[:, :, :].rearrange("p g f -> p (g f)")

        V_ps = bank[0][:, 0:CH]
        H_ps = bank[1][:, 0:CH]
        ST_ps = bank[2][:, 0:CH].rearrange("p (t f) -> p t f", t=TILES)
        M_ps = [bank[3 + c][:, 0:CH].rearrange("p (t f) -> p t f", t=TILES) for c in K2]
        Y_ps = [bank[5 + c][:, 0:CH].rearrange("p (t f) -> p t f", t=TILES) for c in K2]
        O_ps = bank[7][:, 0:P]

        s_const = sem("const_loaded")
        s_mask = sem("mask_loaded")
        s_setp = sem("pool_setup_done")
        s_v = sem("vector_setup_steps")
        s_setv = sem("vector_setup_done")

        x_loaded = [sem(f"x_loaded{k}") for k in K2]
        a_loaded = [sem(f"a_loaded{k}") for k in K2]
        at_loaded = [sem(f"at_loaded{k}") for k in K2]
        names = ["a0_ready", "deg_done", "rs0_done", "rsafe_ready", "rsq_ready", "dis0_done", "dis_ready",
                 "hT_psum", "hT_ready", "u_psum", "rT_ready", "y_psum", "mask_ready",
                 "t0_done", "stats0", "var0", "std0", "rstd0", "x1_ready",
                 "x1T_psum", "x1T_ready", "pR_psum", "R_ready", "pb_done", "q_psum", "z_done",
                 "t1_done", "stats1", "var1", "std1", "rstd1", "x2_ready",
                 "x2T_psum", "x2T_ready", "s_psum", "s_ready", "o_psum", "xb0_done", "sdis_done", "xb_ready",
                 "t2_done", "stats2", "var2", "std2", "rstd2", "x3_ready",
                 "x3T_psum", "x3T_ready", "hh_psum", "hi_ready", "hj_ready",
                 "isedge_done", "edges_counted", "bdeg_done", "res_ready"]
        s = {n: sem(n) for n in names}
        stored = [sem(f"group_stored{k}") for k in K2]

        cnt_ready = sem("cnt_ready")
        count_psum = sem("count_psum")
        most_done = sem("most_done")
        end_ready = sem("end_ready")
        most_ready = sem("most_ready")

        ga_loaded = [sem(f"ga_loaded{q}") for q in K2]
        gh_loaded = [sem(f"gh_loaded{q}") for q in K2]
        gres_loaded = [sem(f"gres_loaded{q}") for q in K2]
        b = {n: sem("e_" + n) for n in
             ["split_up", "split_done", "nz_done", "rank_done", "pos_ready", "below_done", "S_ready", "V_psum", "T_ready",
              "H_psum", "hT_ready", "M_psum", "ST_ready", "Y_psum", "sq_ready", "y_ready",
              "ssum_ready", "sd_ready", "rstd_done", "WS_ready", "O_psum",
              "gamma_done", "t_done", "stats_done", "var_ready", "ostd_ready", "orstd_done", "out_ready",
              "shifted", "acc_done"]}
        out_stored = [sem(f"out_stored{q}") for q in K2]
    
        SLOT_STORED = GROUPS // 2 * 3 * 16 + 1

        block = ctx.enter_context(nc.Block())

        @block.sync
        def _(sp):
            sp.dma_start(const[:, :], const_d).then_inc(s_const, 16)
            sp.dma_start(mask8[:, :], mask_d).then_inc(s_mask, 16)

            def load(dst, src, group, sm):
                sp.dma_start(flat(dst), src[bass.ds(group, 1), :, :].rearrange("o p c -> p (o c)")).then_inc(sm, 16)

            for k in K2:
                load(A[k], a_d, k, a_loaded[k])
                load(X[k], x_d, k, x_loaded[k])
                load(AT[k], at_d, k, at_loaded[k])

            def group_step(it, more):
                for k in K2:
                    n = 2 * it + k + 1
                    if more:
                        sp.wait_ge(s["t0_done"], n)
                        load(X[k], x_d, 2 * it + 2 + k, x_loaded[k])
                for k in K2:
                    n = 2 * it + k + 1
                    if more:
                        sp.wait_ge(s["z_done"], n)
                        sp.wait_ge(s["isedge_done"], n)
                        load(A[k], a_d, 2 * it + 2 + k, a_loaded[k])
                for k in K2:
                    n = 2 * it + k + 1
                    if more:
                        sp.wait_ge(s["t2_done"], n)
                        load(AT[k], at_d, 2 * it + 2 + k, at_loaded[k])
                for k in K2:
                    n = 2 * it + k + 1
                    for buf, dst, ready in ((res, res_s, "res_ready"), (hi, hi_s, "hi_ready"), (hj, hj_s, "hj_ready")):
                        sp.wait_ge(s[ready], n)
                        sp.dma_start(dst[bass.ds(4 * (2 * it + k), GROUP), :, :].rearrange("g p f -> p g f"),
                                     buf[k][:, :, :]).then_inc(stored[k], 16)

            with sp.Fori(0, GROUPS // 2 - 1) as it:
                group_step(it, True)
            group_step(GROUPS // 2 - 1, False)
            for k in K2:
                sp.wait_ge(stored[k], SLOT_STORED)

            def load_a(g, q):
                sp.dma_start(gA[q][:, :], a_g[bass.ds(g, 1), :, :].rearrange("o p c -> p (o c)")).then_inc(ga_loaded[q], 16)

            def load_h(g, q):
                for part_of, src in enumerate((hi_s, hj_s, at_g)):
                    sp.dma_start(gH[q][:, part_of, :], src[bass.ds(g, 1), :, :].rearrange("o p c -> p (o c)")).then_inc(gh_loaded[q], 16)

            def load_res(g, q):
                sp.dma_start(gRES[q][:, :], res_s[bass.ds(g, 1), :, :].rearrange("o p c -> p (o c)")).then_inc(gres_loaded[q], 16)

            def store(g, q, n):
                sp.wait_ge(b["out_ready"], n)
                sp.dma_start(out_d[bass.ds(g, 1), :, :].rearrange("o p c -> p (o c)"), y4[q][:, :]).then_inc(out_stored[q], 16)

            sp.wait_ge(most_ready, 1)
            fullest = sp.value_load(most_i[0:1, 0:1], min_val=0, max_val=P * P)
            with sp.If(fullest > CAPACITY):
                with sp.Fori(0, B) as g:
                    load_a(g, 0)
                    load_h(g, 0)
                    load_res(g, 0)
                    store(g, 0, g + 1)
                sp.wait_ge(out_stored[0], 16 * B + 1)
            with sp.Else():
                for q in K2:
                    load_a(q, q)
                    load_h(q, q)
                    load_res(q, q)

                def pair_step(p, first, more):
                    for q in K2:
                        g = 2 * p + q
                        if more:
                            sp.wait_ge(b["split_done"], g + 1)
                            load_h(g + 2, q)
                            sp.wait_ge(b["nz_done"], g + 1)
                            load_a(g + 2, q)
                    if not first:
                        for q in K2:
                            g = 2 * p + q
                            sp.wait_ge(b["t_done"], g - 1)
                            load_res(g, q)
                            store(g - 2, q, g - 1)

                pair_step(0, True, True)
                with sp.Fori(1, B // 2 - 1) as p:
                    pair_step(p, False, True)
                pair_step(B // 2 - 1, False, False)
                store(B - 2, 0, B - 1)
                store(B - 1, 1, B)
                for q in K2:
                    sp.wait_ge(out_stored[q], 8 * B + 1)

        @block.gpsimd
        def _(pool):
            nc.gpsimd.memset(zeros[:, :], 0.0)
            nc.gpsimd.memset(ident[:, :], 0.0)
            nc.gpsimd.memset(ones_b[:, :], 1.0)
            nc.gpsimd.memset(tri[:, :], 1.0)
            nc.gpsimd.memset(eps_col[:, :], LN_EPS)
            nc.gpsimd.memset(bias0[:, :, :], 0.0)
            nc.gpsimd.memset(bias3[:, :, :], 0.0)
            nc.gpsimd.iota(edge_i[:, :], pattern=[[1, CAPACITY]], base=0, channel_multiplier=0).then_inc(s_setp, 1)
            pool.wait_ge(s_setp, 1)
            nc.gpsimd.affine_select(out=ident[:, :], in_=ident[:, :], compare_op=ALU.not_equal, fill=1.0,
                                    base=0, pattern=[[-1, P]], channel_multiplier=1)
            nc.gpsimd.affine_select(out=tri[:, :], in_=tri[:, :], compare_op=ALU.is_ge, fill=0.0,
                                    base=0, pattern=[[1, P]], channel_multiplier=-1).then_inc(s_setp, 1)
            pool.wait_ge(s_setv, 1)
            beta = C["beta"]
            with pool.Fori(0, GROUPS // 2) as it:
                for k in K2:
                    n = 2 * it + k + 1
                    nc.gpsimd.tensor_copy(maskg[k][:, :], mask[:, bass.ds(4 * (2 * it + k), GROUP)]).then_inc(s["mask_ready"], 1)
                for k in K2:
                    n = 2 * it + k + 1
                    pool.wait_ge(s["deg_done"], n)
                    nc.gpsimd.tensor_tensor(bdeg[k][:, :, :], beta.unsqueeze(1).to_broadcast([P, GROUP, P]),
                                            deg[k][:, :].unsqueeze(2).to_broadcast([P, GROUP, P]), ALU.mult).then_inc(s["bdeg_done"], 1)
                for k in K2:
                    n = 2 * it + k + 1
                    pool.wait_ge(s["x2_ready"], n)
                    nc.gpsimd.tensor_tensor(xb0[k][:, :, :], xn[1][k][:, :, :],
                                            C["L2_b"].unsqueeze(1).to_broadcast([P, GROUP, P]), ALU.add).then_inc(s["xb0_done"], 1)
                for k in K2:
                    n = 2 * it + k + 1
                    pool.wait_ge(s["s_ready"], n)
                    nc.gpsimd.tensor_tensor(sdis[k][:, :, :], ssb[k][:, :, :],
                                            dis[k][:, :].unsqueeze(2).to_broadcast([P, GROUP, P]), ALU.mult).then_inc(s["sdis_done"], 1)
                    pool.wait_ge(s["sdis_done"], n)
                    pool.wait_ge(s["xb0_done"], n)
                    nc.gpsimd.tensor_tensor(xb[k][:, :, :], xb0[k][:, :, :], sdis[k][:, :, :], ALU.add).then_inc(s["xb_ready"], 1)
                for k in K2:
                    n = 2 * it + k + 1
                    pool.wait_ge(s["x3_ready"], n)
                    pool.wait_ge(s["bdeg_done"], n)
                    pool.wait_ge(stored[k], 48 * it + 1)
                    nc.gpsimd.tensor_tensor(res[k][:, :, :], xn[2][k][:, :, :], bdeg[k][:, :, :], ALU.add).then_inc(s["res_ready"], 1)
                pool.wait_ge(s["res_ready"], 2 * it + 2)

            def split_up(q, g, loads):
                pool.wait_ge(gh_loaded[q], loads)
                nc.gpsimd.tensor_tensor(gHu[q][:, :, :], gH[q][:, :, :],
                                        zeros[:, :].unsqueeze(1).to_broadcast([P, 3, P]), ALU.add).then_inc(b["split_up"], 1)
                pool.wait_ge(b["split_up"], g + 1)
                nc.gpsimd.tensor_tensor(gHl[q][:, :, :], gH[q][:, :, :], gHu[q][:, :, :].bitcast(f32),
                                        ALU.subtract).then_inc(b["split_done"], 1)

            def add_residual(q, g, loads):
                pool.wait_ge(gres_loaded[q], loads)
                pool.wait_ge(b["gamma_done"], g + 1)
                nc.gpsimd.tensor_tensor(tout[q][:, :], gout[q][:, :], gRES[q][:, :], ALU.add).then_inc(b["t_done"], 1)

            pool.wait_ge(most_ready, 1)
            fullest = pool.value_load(most_i[0:1, 0:1], min_val=0, max_val=P * P)
            with pool.If(fullest > CAPACITY):
                with pool.Fori(0, B) as g:
                    split_up(0, g, 48 * g + 48)
                    add_residual(0, g, 16 * g + 16)
            with pool.Else():
                split_up(0, 0, 48)
                split_up(1, 1, 48)
                with pool.Fori(1, B // 2) as p:
                    for q in K2:
                        g = 2 * p + q
                        pool.wait_ge(b["M_psum"], 2 * g - 2)
                        split_up(q, g, 48 * p + 48)
                        add_residual(q, g - 2, 16 * p)
                for q in K2:
                    add_residual(q, B - 2 + q, 8 * B)

        @block.scalar
        def _(act):
            nc.scalar.preload_act_table(ACT.Sqrt)
            act.wait_ge(s_const, 16)
            act.wait_ge(s_setp, 2)

            def ln_std(k, n, layer):
                act.wait_ge(s[f"var{layer}"], n)
                nc.scalar.activation(std[k][:, :], mv[k][:, :, 1], ACT.Sqrt, bias=eps_col[:, 0:1]).then_inc(s[f"std{layer}"], 1)

            def evict(k, n, ps, dst, wait, done, func=ACT.Copy, **kw):
                act.wait_ge(s[wait], n)
                nc.scalar.activation(dst[k][:, :, :], ps, func, **kw).then_inc(s[done], 1)

            with act.Fori(0, GROUPS // 2) as it:
                ns = [2 * it + 1, 2 * it + 2]
                for k, n in enumerate(ns):
                    evict(k, n, psA(k, 0), tmpT, "hT_psum", "hT_ready")
                for k, n in enumerate(ns):
                    act.wait_ge(s["rsafe_ready"], n)
                    nc.scalar.activation(rsq[k][:, :], rsafe[k][:, :], ACT.Sqrt).then_inc(s["rsq_ready"], 1)
                for k, n in enumerate(ns):
                    evict(k, n, psA(k, 1), rT, "u_psum", "rT_ready", ACT.Relu, bias=C["L0_b1"])
                for k, n in enumerate(ns):
                    ln_std(k, n, 0)
                for k, n in enumerate(ns):
                    evict(k, n, psA(k, 1), tmpT, "x1T_psum", "x1T_ready")
                for k, n in enumerate(ns):
                    evict(k, n, psA(k, 3), R, "pR_psum", "R_ready")
                for k, n in enumerate(ns):
                    ln_std(k, n, 1)
                for k, n in enumerate(ns):
                    evict(k, n, psA(k, 1), tmpT, "x2T_psum", "x2T_ready")
                for k, n in enumerate(ns):
                    ln_std(k, n, 2)
                for k, n in enumerate(ns):
                    evict(k, n, psA(k, 1), tmpT, "x3T_psum", "x3T_ready")
                for k, n in enumerate(ns):
                    act.wait_ge(stored[k], 48 * it + 1)
                    evict(k, n, psA(k, 3), hj, "hh_psum", "hj_ready")

            def relu(c, n):
                act.wait_ge(b["H_psum"], n)
                nc.scalar.activation(hT[c][:, :], H_ps, ACT.Relu).then_inc(b["hT_ready"], 1)

            def starts(c, n):
                act.wait_ge(b["M_psum"], n)
                nc.scalar.activation(ST[c][:, :, :], ST_ps, ACT.Copy).then_inc(b["ST_ready"], 1)

            def spread(n):
                act.wait_ge(b["ssum_ready"], n)
                nc.scalar.activation(esd[:, :], ssum[:, :], ACT.Sqrt, bias=eps_col[:, 0:1], scale=invp).then_inc(b["sd_ready"], 1)

            def square(c, n):
                act.wait_ge(b["Y_psum"], n)
                nc.scalar.activation(sq[c][:, :, :], Y_ps[c], ACT.Square).then_inc(b["sq_ready"], 1)
                nc.scalar.activation(ysb[c][:, :, :], Y_ps[c], ACT.Copy).then_inc(b["y_ready"], 1)

            def out_std(q, n):
                act.wait_ge(b["var_ready"], n)
                nc.scalar.activation(ostd[q][:, :], omv[q][:, 1:2], ACT.Sqrt, bias=eps_col[:, 0:1]).then_inc(b["ostd_ready"], 1)

            act.wait_ge(most_ready, 1)
            fullest = act.value_load(most_i[0:1, 0:1], min_val=0, max_val=P * P)
            with act.If(fullest > CAPACITY):
                with act.Fori(0, B) as g:
                    with act.Fori(0, ALL_CHUNKS) as c:
                        n = g * ALL_CHUNKS + c + 1
                        relu(0, n)
                        starts(0, n)
                        square(0, n)
                        spread(n)
                    out_std(0, g + 1)
            with act.Else():
                def pair_step(p, first):
                    for q in K2:
                        g = 2 * p + q
                        for c in K2:
                            n = 2 * g + c + 1
                            relu(c, n)
                            if not (first and q == 0 and c == 0):
                                spread(n - 1)
                            starts(c, n)
                            if c == 1 and not first:
                                out_std(q, g - 1)
                            square(c, n)

                pair_step(0, True)
                with act.Fori(1, B // 2) as p:
                    pair_step(p, False)
                spread(2 * B)
                for q in K2:
                    out_std(q, B - 1 + q)

        @block.vector
        def _(dve):
            step = [0]

            def then(ins):
                ins.then_inc(s_v, 1)
                step[0] += 1
                dve.wait_ge(s_v, step[0])

            dve.wait_ge(s_setp, 2)
            dve.wait_ge(s_const, 16)
            dve.wait_ge(s_mask, 16)
            nc.vector.tensor_copy(mask[:, :], mask8[:, :])
            nc.vector.tensor_copy(edge[:, :], edge_i[:, :])
            then(nc.vector.tensor_scalar(w2mean[:, :], C["L0_eps"], 1.0, None, ALU.add))
            then(nc.vector.tensor_scalar(scaled_id[:, :], ident[:, :], w2mean[:, 0:1], None, ALU.mult))
            nc.vector.tensor_scalar(edge1[:, :], edge[:, :], 1.0, None, ALU.add)
            nc.vector.tensor_reduce(b2mean[:, :], C["L3_b2"], AX.X, ALU.add)
            then(nc.vector.tensor_reduce(w2mean[:, :], C["L3_W2"], AX.X, ALU.add))
            nc.vector.tensor_scalar(b2mean[:, :], b2mean[:, :], invp, None, ALU.mult)
            then(nc.vector.tensor_scalar(w2mean[:, :], w2mean[:, :], invp, None, ALU.mult))
            nc.vector.tensor_scalar(b2c[:, :], C["L3_b2"], b2mean[:, 0:1], None, ALU.subtract)
            then(nc.vector.tensor_scalar(w2c[:, :], C["L3_W2"], w2mean[:, 0:1], None, ALU.subtract))
            for row, bias, copies, m in ((C["L0_b2"], bias0, GROUP, 0), (b2c[:, :], bias3, TILES, 3)):
                then(nc.vector.tensor_copy(part[m][:, :], row))
                then(nc.vector.tensor_tensor(split[0][:, :], row, part[m][:, :], ALU.subtract))
                then(nc.vector.tensor_copy(part[m + 1][:, :], split[0][:, :]))
                then(nc.vector.tensor_tensor(split[1][:, :], split[0][:, :], part[m + 1][:, :], ALU.subtract))
                then(nc.vector.tensor_copy(part[m + 2][:, :], split[1][:, :]))
                for r in range(3):
                    for c in range(copies):
                        last = nc.vector.tensor_copy(bias[32 * r:32 * r + 1, c, :], part[m + r][32 * r:32 * r + 1, :])
                then(last)
            for i, counter in enumerate(stored + out_stored):
                nc.vector.memset(seeds[:, i:i + 1], 0.0).then_inc(counter, 1)
            nc.vector.memset(ssum[:, :], 0.0).then_inc(s_setv, 1)

            def ln_stats(k, n, layer):
                dve.wait_ge(s[f"t{layer}_done"], n)
                for g in range(GROUP):
                    last = nc.vector.bn_stats(stats[k][:, g, :], t[k][:, g, :])
                last.then_inc(s[f"stats{layer}"], 1)

            def ln_var(k, n, layer):
                dve.wait_ge(s_const, 16)
                dve.wait_ge(s[f"stats{layer}"], n)
                for g in range(GROUP):
                    last = nc.vector.bn_aggr(mv[k][:, g, :], stats[k][:, g, :])
                last.then_inc(s[f"var{layer}"], 1)

            def ln_rstd(k, n, layer):
                dve.wait_ge(s[f"std{layer}"], n)
                nc.vector.reciprocal(rstd[k][:, :], std[k][:, :]).then_inc(s[f"rstd{layer}"], 1)

            def ln_apply(k, n, layer):
                dve.wait_ge(s[f"rstd{layer}"], n)
                for g in range(GROUP):
                    last = nc.vector.tensor_scalar(xn[layer][k][:, g, :], t[k][:, g, :], mv[k][:, g, 0:1],
                                                   rstd[k][:, g:g + 1], ALU.subtract, ALU.mult)
                last.then_inc(s[f"x{layer + 1}_ready"], 1)

            def layer_norm(ns, layer):
                for stage in (ln_stats, ln_var, ln_rstd, ln_apply):
                    for k, n in enumerate(ns):
                        stage(k, n, layer)

            with dve.Fori(0, GROUPS // 2) as it:
                ns = [2 * it + 1, 2 * it + 2]
                for k, n in enumerate(ns):
                    dve.wait_ge(a_loaded[k], 16 * it + 16)
                    nc.vector.tensor_tensor(A0[k][:, :, :], A[k][:, :, :],
                                            scaled_id[:, :].unsqueeze(1).to_broadcast([P, GROUP, P]), ALU.add).then_inc(s["a0_ready"], 1)
                for k, n in enumerate(ns):
                    nc.vector.tensor_reduce(deg[k][:, :], A[k][:, :, :], AX.X, ALU.add).then_inc(s["deg_done"], 1)
                for k, n in enumerate(ns):
                    dve.wait_ge(s["deg_done"], n)
                    nc.vector.reciprocal(rdeg[k][:, :], deg[k][:, :])
                    nc.vector.tensor_scalar(rs0[k][:, :], deg[k][:, :], 1.0, 0.0, ALU.add, ALU.is_equal).then_inc(s["rs0_done"], 1)
                for k, n in enumerate(ns):
                    dve.wait_ge(s["rs0_done"], n)
                    nc.vector.scalar_tensor_tensor(rsafe[k][:, :], deg[k][:, :], 1.0, rs0[k][:, :], ALU.add, ALU.add).then_inc(s["rsafe_ready"], 1)
                for k, n in enumerate(ns):
                    dve.wait_ge(s["rsq_ready"], n)
                    nc.vector.reciprocal(dis0[k][:, :], rsq[k][:, :]).then_inc(s["dis0_done"], 1)
                for k, n in enumerate(ns):
                    dve.wait_ge(s["dis0_done"], n)
                    nc.vector.scalar_tensor_tensor(dis[k][:, :], rs0[k][:, :], 0.0, dis0[k][:, :], ALU.is_equal, ALU.mult).then_inc(s["dis_ready"], 1)
                for k, n in enumerate(ns):
                    dve.wait_ge(s["mask_ready"], n)
                    dve.wait_ge(x_loaded[k], 16 * it + 16)
                    dve.wait_ge(s["y_psum"], n)
                    for g in range(GROUP):
                        last = nc.vector.scalar_tensor_tensor(t[k][:, g, :], psA(k, 0)[:, g, :], maskg[k][:, g:g + 1],
                                                              X[k][:, g, :], ALU.mult, ALU.add)
                    last.then_inc(s["t0_done"], 1)
                layer_norm(ns, 0)
                for k, n in enumerate(ns):
                    nc.vector.tensor_scalar(isedge[k][:, :, :], A[k][:, :, :], 0.0, None, ALU.not_equal).then_inc(s["isedge_done"], 1)
                for k, n in enumerate(ns):
                    dve.wait_ge(s["isedge_done"], n)
                    nc.vector.tensor_reduce(cntf[:, bass.ds(4 * (2 * it + k), GROUP)], isedge[k][:, :, :], AX.X, ALU.add).then_inc(s["edges_counted"], 1)
                for k, n in enumerate(ns):
                    dve.wait_ge(s["pR_psum"], n)
                    nc.vector.tensor_tensor(pb[k][:, :, :], psA(k, 2), C["L1_b"].unsqueeze(1).to_broadcast([P, GROUP, P]), ALU.add).then_inc(s["pb_done"], 1)
                for k, n in enumerate(ns):
                    dve.wait_ge(s["q_psum"], n)
                    dve.wait_ge(s["pb_done"], n)
                    for g in range(GROUP):
                        last = nc.vector.scalar_tensor_tensor(z[k][:, g, :], psA(k, 0)[:, g, :], rdeg[k][:, g:g + 1],
                                                              pb[k][:, g, :], ALU.mult, ALU.add)
                    last.then_inc(s["z_done"], 1)
                for k, n in enumerate(ns):
                    dve.wait_ge(s["z_done"], n)
                    nc.vector.scalar_tensor_tensor(flat(t[k]), flat(z[k]), 0.0, flat(xn[0][k]), ALU.max, ALU.add).then_inc(s["t1_done"], 1)
                layer_norm(ns, 1)
                for k, n in enumerate(ns):
                    dve.wait_ge(s["s_psum"], n)
                    dve.wait_ge(s["dis_ready"], n)
                    nc.vector.tensor_tensor(ssb[k][:, :, :], psA(k, 2), dis[k][:, :].unsqueeze(2).to_broadcast([P, GROUP, P]), ALU.mult).then_inc(s["s_ready"], 1)
                for k, n in enumerate(ns):
                    dve.wait_ge(s["o_psum"], n)
                    dve.wait_ge(s["xb_ready"], n)
                    for g in range(GROUP):
                        last = nc.vector.scalar_tensor_tensor(t[k][:, g, :], psA(k, 0)[:, g, :], dis[k][:, g:g + 1],
                                                              xb[k][:, g, :], ALU.mult, ALU.add)
                    last.then_inc(s["t2_done"], 1)
                layer_norm(ns, 2)
                for k, n in enumerate(ns):
                    dve.wait_ge(s["hh_psum"], n)
                    dve.wait_ge(stored[k], 48 * it + 1)
                    nc.vector.tensor_tensor(hi[k][:, :, :], psA(k, 2), C["L3_b1"].unsqueeze(1).to_broadcast([P, GROUP, P]), ALU.add).then_inc(s["hi_ready"], 1)

            dve.wait_ge(s["edges_counted"], GROUPS)
            nc.vector.tensor_copy(cnt[:, :], cntf[:, :]).then_inc(cnt_ready, 1)
            dve.wait_ge(count_psum, 1)
            nc.vector.tensor_copy(end[:, :], bank[0][:, 0:B]).then_inc(end_ready, 1)
            nc.vector.tensor_reduce(most[0:1, :], bank[1][0:1, 0:B], AX.X, ALU.max).then_inc(most_done, 1)
            dve.wait_ge(end_ready, 1)
            nc.vector.tensor_tensor(off[:, :], end[:, :], cntf[:, :], ALU.subtract).then_inc(end_ready, 1)
            dve.wait_ge(most_done, 1)
            nc.vector.tensor_copy(most_i[0:1, :], most[0:1, :]).then_inc(most_ready, 1)

            def edges(q, g, loads):
                dve.wait_ge(ga_loaded[q], loads)
                nc.vector.tensor_scalar(nz[q][:, :], gA[q][:, :], 0.0, None, ALU.not_equal).then_inc(b["nz_done"], 1)

            def ranks(q, g):
                dve.wait_ge(b["nz_done"], g + 1)
                nc.vector.tensor_tensor_scan(rank[q][:, :], nz[q][:, :], zeros[:, :], 0.0, ALU.add, ALU.add).then_inc(b["rank_done"], 1)

            def bounds(q, g):
                nc.vector.tensor_scalar(below[q][:, :], edge[:, :], end[:, bass.ds(g, 1)], None, ALU.is_lt).then_inc(b["below_done"], 1)

            def starts(q, g):
                dve.wait_ge(b["below_done"], g + 1)
                nc.vector.scalar_tensor_tensor(S[q][:, :], edge[:, :], off[:, bass.ds(g, 1)], below[q][:, :],
                                               ALU.is_ge, ALU.mult).then_inc(b["S_ready"], 1)

            def places(q, g):
                dve.wait_ge(b["rank_done"], g + 1)
                nc.vector.scalar_tensor_tensor(pos[q][:, :], rank[q][:, :], off[:, bass.ds(g, 1)], nz[q][:, :],
                                               ALU.add, ALU.mult).then_inc(b["pos_ready"], 1)

            def ends(c, e0, n):
                dve.wait_ge(b["V_psum"], n)
                nc.vector.tensor_tensor(T[c][:, :], V_ps, edge1[:, e0:e0 + CH], ALU.is_equal).then_inc(b["T_ready"], 1)

            def sum_squares(c, n):
                dve.wait_ge(b["sq_ready"], n)
                nc.vector.tensor_reduce(ssum[:, :], sq[c][:, :, :], AX.X, ALU.add).then_inc(b["ssum_ready"], 1)

            def invert(n):
                dve.wait_ge(b["sd_ready"], n)
                nc.vector.reciprocal(erstd[:, :], esd[:, :]).then_inc(b["rstd_done"], 1)

            def weigh(c, n):
                dve.wait_ge(b["rstd_done"], n)
                dve.wait_ge(b["ST_ready"], n)
                for i in range(TILES):
                    last = nc.vector.scalar_tensor_tensor(WS[c][:, i, :], M_ps[c][:, i, :], erstd[:, i:i + 1],
                                                          ST[c][:, i, :], ALU.mult, ALU.mult)
                last.then_inc(b["WS_ready"], 1)

            def scale_sum(q, src):
                nc.vector.tensor_tensor(gout[q][:, :], src, C["gamma"], ALU.mult).then_inc(b["gamma_done"], 1)

            def norm_stats(q, g):
                dve.wait_ge(b["t_done"], g + 1)
                nc.vector.bn_stats(ostats[q][:, :], tout[q][:, :]).then_inc(b["stats_done"], 1)

            def norm_var(q, g):
                dve.wait_ge(s_const, 16)
                dve.wait_ge(b["stats_done"], g + 1)
                nc.vector.bn_aggr(omv[q][:, :], ostats[q][:, :]).then_inc(b["var_ready"], 1)

            def norm_rstd(q, g):
                dve.wait_ge(b["ostd_ready"], g + 1)
                nc.vector.reciprocal(orstd[q][:, :], ostd[q][:, :]).then_inc(b["orstd_done"], 1)

            def norm_apply(q, g, stores):
                dve.wait_ge(b["orstd_done"], g + 1)
                dve.wait_ge(out_stored[q], stores)
                nc.vector.tensor_scalar(y4[q][:, :], tout[q][:, :], omv[q][:, 0:1], orstd[q][:, 0:1],
                                        ALU.subtract, ALU.mult).then_inc(b["out_ready"], 1)

            dve.wait_ge(most_ready, 1)
            dve.wait_ge(end_ready, 2)
            fullest = dve.value_load(most_i[0:1, 0:1], min_val=0, max_val=P * P)
            with dve.If(fullest > CAPACITY):
                with dve.Fori(0, B) as g:
                    edges(0, g, 16 * g + 16)
                    nc.vector.tensor_copy(goff[:, :], off[:, bass.ds(g, 1)])
                    nc.vector.tensor_copy(gend[:, :], end[:, bass.ds(g, 1)])
                    nc.vector.memset(acc[:, :], 0.0)
                    ranks(0, g)
                    dve.wait_ge(b["rank_done"], g + 1)
                    nc.vector.scalar_tensor_tensor(pos32[:, :], rank[0][:, :], goff[:, 0:1], nz[0][:, :],
                                                   ALU.add, ALU.mult).then_inc(b["shifted"], 1)
                    with dve.Fori(0, ALL_CHUNKS) as c:
                        n = g * ALL_CHUNKS + c + 1
                        dve.wait_ge(b["shifted"], n + g)
                        nc.vector.tensor_copy(pos[0][:, :], pos32[:, :]).then_inc(b["pos_ready"], 1)
                        nc.vector.tensor_scalar(below[0][:, 0:CH], edge[:, 0:CH], gend[:, 0:1], None, ALU.is_lt).then_inc(b["below_done"], 1)
                        dve.wait_ge(b["below_done"], n)
                        nc.vector.scalar_tensor_tensor(S[0][:, 0:CH], edge[:, 0:CH], goff[:, 0:1], below[0][:, 0:CH],
                                                       ALU.is_ge, ALU.mult).then_inc(b["S_ready"], 1)
                        ends(0, 0, n)
                        sum_squares(0, n)
                        invert(n)
                        weigh(0, n)
                        dve.wait_ge(b["S_ready"], n)
                        nc.vector.tensor_scalar(pos32[:, :], pos32[:, :], float(CH), None, ALU.subtract)
                        nc.vector.tensor_scalar(goff[:, :], goff[:, :], float(CH), None, ALU.subtract)
                        nc.vector.tensor_scalar(gend[:, :], gend[:, :], float(CH), None, ALU.subtract).then_inc(b["shifted"], 1)
                        dve.wait_ge(b["O_psum"], n)
                        nc.vector.tensor_tensor(acc[:, :], acc[:, :], O_ps, ALU.add).then_inc(b["acc_done"], 1)
                        dve.wait_ge(b["acc_done"], n)
                    scale_sum(0, acc[:, :])
                    norm_stats(0, g)
                    norm_var(0, g)
                    norm_rstd(0, g)
                    norm_apply(0, g, 16 * g + 1)
            with dve.Else():
                def pair_step(p, first, last):
                    for q in K2:
                        g = 2 * p + q
                        final = last and q == 1
                        for c in K2:
                            n = 2 * g + c + 1
                            if c == 0:
                                ends(1, CH, n + 1)
                                if not first:
                                    dve.wait_ge(b["O_psum"], g - 1)
                                    scale_sum(q, O_ps)
                                if not final:
                                    edges(1 - q, g + 1, 16 * (p + q) + 16)
                                    bounds(1 - q, g + 1)
                                    ranks(1 - q, g + 1)
                                    starts(1 - q, g + 1)
                                    places(1 - q, g + 1)
                                if not (first and q == 0):
                                    sum_squares(1, n - 1)
                                    invert(n - 1)
                                    weigh(1, n - 1)
                            else:
                                if not final:
                                    ends(0, 0, n + 1)
                                if not first:
                                    norm_stats(q, g - 2)
                                sum_squares(0, n - 1)
                                if not first:
                                    norm_var(q, g - 2)
                                invert(n - 1)
                                weigh(0, n - 1)
                                if not first:
                                    norm_rstd(q, g - 2)
                                    norm_apply(q, g - 2, 16 * (p - 1) + 1)

                edges(0, 0, 16)
                bounds(0, 0)
                ranks(0, 0)
                starts(0, 0)
                places(0, 0)
                ends(0, 0, 1)
                pair_step(0, True, False)
                with dve.Fori(1, B // 2 - 1) as p:
                    pair_step(p, False, False)
                pair_step(B // 2 - 1, False, True)
                dve.wait_ge(b["O_psum"], B - 1)
                scale_sum(0, O_ps)
                sum_squares(1, 2 * B)
                invert(2 * B)
                weigh(1, 2 * B)
                dve.wait_ge(b["O_psum"], B)
                scale_sum(1, O_ps)
                for q in K2:
                    norm_stats(q, B - 2 + q)
                    norm_var(q, B - 2 + q)
                for q in K2:
                    norm_rstd(q, B - 2 + q)
                    norm_apply(q, B - 2 + q, 8 * B - 15)

        @block.tensor
        def _(pe):
            pe.wait_ge(s_setv, 1)
            pe.wait_ge(s_setp, 2)

            def products(k, bk, lhs, rhs, done, bias=None):
                if bias is not None:
                    nc.tensor.matmul(flat(psA(k, bk)), ones_b[:, :], flat(bias), start=True, stop=False)
                for g in range(GROUP):
                    last = nc.tensor.matmul(psA(k, bk)[:, g, :], lhs(g), rhs(g), start=bias is None,
                                            stop=bias is None or g == GROUP - 1)
                if done:
                    last.then_inc(s[done], 1)

            def transposes(k, src, done):
                for g in range(GROUP):
                    last = nc.tensor.transpose(psA(k, 1)[:, g, :], src[k][:, g, :], ident[:, :])
                last.then_inc(s[done], 1)

            with pe.Fori(0, GROUPS // 2) as it:
                ns = [2 * it + 1, 2 * it + 2]
                for k, n in enumerate(ns):
                    pe.wait_ge(s["a0_ready"], n)
                    pe.wait_ge(x_loaded[k], 16 * it + 16)
                    products(k, 0, lambda g: X[k][:, g, :], lambda g: A0[k][:, g, :], "hT_psum")
                for k, n in enumerate(ns):
                    pe.wait_ge(s["hT_ready"], n)
                    nc.tensor.matmul(flat(psA(k, 1)), C["L0_W1"], flat(tmpT[k]), start=True, stop=True).then_inc(s["u_psum"], 1)
                for k, n in enumerate(ns):
                    pe.wait_ge(s["rT_ready"], n)
                    products(k, 0, lambda g: rT[k][:, g, :], lambda g: C["L0_W2"], "y_psum", bias=bias0)
                for k, n in enumerate(ns):
                    pe.wait_ge(s["x1_ready"], n)
                    transposes(k, xn[0], "x1T_psum")
                for k, n in enumerate(ns):
                    pe.wait_ge(s["x1T_ready"], n)
                    products(k, 3, lambda g: tmpT[k][:, g, :], lambda g: C["L1_WbT"], None)
                    products(k, 2, lambda g: tmpT[k][:, g, :], lambda g: C["L1_WaT"], "pR_psum")
                for k, n in enumerate(ns):
                    pe.wait_ge(s["R_ready"], n)
                    products(k, 0, lambda g: A[k][:, g, :], lambda g: R[k][:, g, :], "q_psum")
                for k, n in enumerate(ns):
                    pe.wait_ge(s["x2_ready"], n)
                    transposes(k, xn[1], "x2T_psum")
                for k, n in enumerate(ns):
                    pe.wait_ge(s["x2T_ready"], n)
                    products(k, 2, lambda g: tmpT[k][:, g, :], lambda g: C["L2_W"], "s_psum")
                for k, n in enumerate(ns):
                    pe.wait_ge(s["s_ready"], n)
                    pe.wait_ge(at_loaded[k], 16 * it + 16)
                    products(k, 0, lambda g: AT[k][:, g, :], lambda g: ssb[k][:, g, :], "o_psum")
                for k, n in enumerate(ns):
                    pe.wait_ge(s["x3_ready"], n)
                    transposes(k, xn[2], "x3T_psum")
                for k, n in enumerate(ns):
                    pe.wait_ge(s["x3T_ready"], n)
                    products(k, 3, lambda g: tmpT[k][:, g, :], lambda g: C["L3_W1b"], None)
                    products(k, 2, lambda g: tmpT[k][:, g, :], lambda g: C["L3_W1a"], "hh_psum")

            pe.wait_ge(cnt_ready, 1)
            pe.wait_ge(s["hj_ready"], GROUPS)
            nc.tensor.matmul(bank[0][:, 0:B], tri[:, :], cnt[:, :], start=True, stop=True)
            nc.tensor.matmul(bank[1][:, 0:B], ones_b[:, :], cnt[:, :], start=True, stop=True).then_inc(count_psum, 1)

            def place(q, c, n_s):
                pe.wait_ge(b["S_ready"], n_s)
                pe.wait_ge(b["pos_ready"], n_s)
                nc.tensor.matmul(V_ps, pos[q][:, :], S[q][:, c * CH:(c + 1) * CH], start=True, stop=True).then_inc(b["V_psum"], 1)

            def gather(q, c, slot, n, g):
                pe.wait_ge(b["T_ready"], n)
                pe.wait_ge(b["split_done"], g + 1)
                for i, half in enumerate((gHu, gHl)):
                    nc.tensor.matmul(H_ps, half[q][:, 0, :], S[q][:, c * CH:(c + 1) * CH], start=i == 0, stop=False)
                for i, half in enumerate((gHu, gHl)):
                    last = nc.tensor.matmul(H_ps, half[q][:, 1, :], T[slot][:, :], start=False, stop=i == 1)
                last.then_inc(b["H_psum"], 1)

            def turn(q, c, n):
                if n is not None:
                    pe.wait_ge(b["ST_ready"], n)
                for i in range(TILES):
                    e0 = c * CH + i * P
                    last = nc.tensor.transpose(ST_ps[:, i, :], S[q][:, e0:e0 + P].bitcast(f32), ident[:, :])

            def rows(q, slot):
                for i in range(TILES):
                    for half in (gHu, gHl):
                        last = nc.tensor.matmul(M_ps[slot][:, i, :], T[slot][:, i * P:(i + 1) * P], half[q][:, 2, :],
                                                start=half is gHu, stop=half is gHl)
                last.then_inc(b["M_psum"], 1)

            def mlp(slot, n):
                pe.wait_ge(b["hT_ready"], n)
                nc.tensor.matmul(Y_ps[slot].rearrange("p t f -> p (t f)"), ones_b[:, :], flat(bias3), start=True, stop=False)
                for i in range(TILES):
                    last = nc.tensor.matmul(Y_ps[slot][:, i, :], hT[slot][:, i * P:(i + 1) * P], w2c[:, :], start=False, stop=i == TILES - 1)
                last.then_inc(b["Y_psum"], 1)

            def scatter(slot, n, start, stop):
                pe.wait_ge(b["WS_ready"], n)
                pe.wait_ge(b["y_ready"], n)
                for i in range(TILES):
                    last = nc.tensor.matmul(O_ps, WS[slot][:, i, :], ysb[slot][:, i, :],
                                            start=start and i == 0, stop=stop and i == TILES - 1)
                if stop:
                    last.then_inc(b["O_psum"], 1)

            pe.wait_ge(most_ready, 1)
            fullest = pe.value_load(most_i[0:1, 0:1], min_val=0, max_val=P * P)
            with pe.If(fullest > CAPACITY):
                with pe.Fori(0, B) as g:
                    with pe.Fori(0, ALL_CHUNKS) as c:
                        n = g * ALL_CHUNKS + c + 1
                        place(0, 0, n)
                        gather(0, 0, 0, n, g)
                        turn(0, 0, None)
                        rows(0, 0)
                        mlp(0, n)
                        scatter(0, n, True, True)
            with pe.Else():
                def pair_step(p, first, last):
                    for q in K2:
                        g = 2 * p + q
                        for c in K2:
                            n = 2 * g + c + 1
                            gather(q, c, c, n, g)
                            turn(q, c, None if first and q == 0 and c == 0 else n - 1)
                            if not (first and q == 0):
                                pe.wait_ge(b["WS_ready"], n - 2)
                            rows(q, c)
                            if not (first and q == 0):
                                if c == 0 and not (first and q == 1):
                                    pe.wait_ge(b["gamma_done"], g - 1)
                                scatter(c, n - 2, c == 0, c == 1)
                            mlp(c, n)
                            if not (last and q == 1):
                                if c == 0:
                                    pe.wait_ge(b["T_ready"], n + 1)
                                    place(1 - q, 0, g + 2)
                                else:
                                    pe.wait_ge(b["T_ready"], n + 1)
                                    place(1 - q, 1, g + 2)

                place(0, 0, 1)
                pe.wait_ge(b["T_ready"], 1)
                place(0, 1, 1)
                pair_step(0, True, False)
                with pe.Fori(1, B // 2 - 1) as p:
                    pair_step(p, False, False)
                pair_step(B // 2 - 1, False, True)
                pe.wait_ge(b["gamma_done"], B - 1)
                scatter(0, 2 * B - 1, True, False)
                scatter(1, 2 * B, False, True)


def kernel(x, adj, nodemask, L0_gnn_W1, L0_gnn_b1, L0_gnn_W2, L0_gnn_b2, L0_gnn_eps, L1_gnn_W, L1_gnn_b,
           L2_gnn_weight, L2_gnn_bias, L3_gnn_W1, L3_gnn_b1, L3_gnn_W2, L3_gnn_b2, L3_gnn_gamma, L3_gnn_beta):
    import numpy as np
    import concourse.bacc as bacc
    from concourse.bass_utils import run_bass_kernel_spmd

    x, adj = np.asarray(x), np.asarray(adj)

    def grouped(a):
        return np.ascontiguousarray(a.reshape(GROUPS, GROUP, P, P).transpose(0, 2, 1, 3).reshape(GROUPS, P, GW))

    adj_t = np.ascontiguousarray(adj.transpose(0, 2, 1))
    w1 = np.asarray(L1_gnn_W)
    w3 = np.asarray(L3_gnn_W1)
    mats = [L0_gnn_W1, L0_gnn_W2, w1[:, :P].T, w1[:, P:].T, L2_gnn_weight, w3[:P], w3[P:], L3_gnn_W2]
    rows = [L0_gnn_b2, L1_gnn_b, L2_gnn_bias, L3_gnn_b1, L3_gnn_b2, L3_gnn_gamma, L3_gnn_beta]
    cols = [np.asarray(L0_gnn_b1).reshape(P, 1), np.broadcast_to(np.asarray(L0_gnn_eps).reshape(1, 1), (P, 1))]
    consts = np.ascontiguousarray(np.concatenate(
        [np.asarray(m) for m in mats] + [np.broadcast_to(np.asarray(r).reshape(1, P), (P, P)) for r in rows] + cols, axis=1))
    arrays = {
        "x_groups": grouped(x), "adj_groups": grouped(adj), "adjT_groups": grouped(adj_t),
        "nodemask_T": np.ascontiguousarray(np.asarray(nodemask).T).view(np.uint8), "constants": consts,
        "adj": np.ascontiguousarray(adj), "adj_T": adj_t,
    }
    nc = bacc.Bacc("TRN2", target_bir_lowering=False, num_devices=1)
    ap = {n: nc.dram_tensor(n, a.shape, mybir.dt.from_np(a.dtype), kind="ExternalInput").ap() for n, a in arrays.items()}
    out = nc.dram_tensor("out", (B, P, P), mybir.dt.float32, kind="ExternalOutput").ap()
    gnn_stack(nc, ap["x_groups"], ap["adj_groups"], ap["adjT_groups"], ap["nodemask_T"], ap["constants"],
              ap["adj"], ap["adj_T"], out)
    r = run_bass_kernel_spmd(nc, [arrays], core_ids=[0])
    return r.results[0]["out"]
```

```python
import concourse.bass as bass
from concourse import mybir
from contextlib import ExitStack

P = 128
B = 64
GROUP = 2
GROUPS = B // GROUP
SLOTS = 4
ROUNDS = GROUPS // SLOTS
PERIOD = 25.60
APART = PERIOD / SLOTS
PERIOD3 = 13.12
GW = GROUP * P
CH = 384
TILES = CH // P
FAST_CHUNKS = 2
CAPACITY = FAST_CHUNKS * CH
ALL_CHUNKS = -(-P * P // CH)
LN_EPS = 1e-5

MATS = ["L0_W1", "L0_W2", "L1_WaT", "L1_WbT", "L2_W", "L3_W1a", "L3_W1b", "L3_W2"]
ROWS = ["L0_b2", "L1_b", "L2_b", "L3_b2", "gamma", "beta"]
COLS = ["L0_b1", "L0_eps", "L3_b1"]
CONST_W = (len(MATS) + len(ROWS)) * P + len(COLS)


def gnn_stack(nc, x_d, a_d, at_d, mask_d, const_d, a_g, at_g, out_d):
    f32, bf16, f16 = mybir.dt.float32, mybir.dt.bfloat16, mybir.dt.float16
    i32, u8 = mybir.dt.int32, mybir.dt.uint8
    f32r = mybir.dt.float32r
    ALU = mybir.AluOpType
    ACT = mybir.ActivationFunctionType
    AX = mybir.AxisListType

    hh_s = nc.dram_tensor("hh_scratch", (B, P, 2 * P), f32).ap()
    res_s = nc.dram_tensor("res_scratch", (B, P, P), f32).ap()

    ctx = ExitStack()
    with ctx:
        def sb(name, shape, dt=f32):
            return ctx.enter_context(nc.sbuf_tensor(name, shape, dt))

        def sem(name):
            return ctx.enter_context(nc.semaphore(name))

        const = sb("const", [P, CONST_W])
        C = {n: const[:, i * P:(i + 1) * P] for i, n in enumerate(MATS + ROWS)}
        at = (len(MATS) + len(ROWS)) * P
        for i, n in enumerate(COLS):
            C[n] = const[:, at + i:at + i + 1]
        ident = sb("ident", [P, P])
        ones_f = sb("ones_f", [P, 1])
        tri = sb("tri", [P, P], bf16)
        diff = sb("diff", [P, P], bf16)
        ones_b = sb("ones_b", [P, P], bf16)
        zeros = sb("zeros", [P, P])
        edge_i = sb("edge_i", [P, CAPACITY], i32)
        edge = sb("edge", [P, CAPACITY], f16)
        edge1 = sb("edge1", [P, CAPACITY])
        scaled_id = sb("scaled_id", [P, P])
        eps_col = sb("eps_col", [P, 1])
        mask8 = sb("mask8", [P, B], u8)
        mask = sb("mask", [P, B])
        seeds = sb("seeds", [P, 8])
        w2mean = sb("w2mean", [P, 1])
        w2c = sb("w2c", [P, P])
        b2mean = sb("b2mean", [P, 1])
        b2c = sb("b2c", [P, P])
        split = [sb(f"split{n}", [P, P]) for n in range(4)]
        part = [sb(f"part{n}", [P, P], bf16) for n in range(9)]
        bias0 = sb("bias0", [P, GROUP, P], bf16)
        bias1 = sb("bias1", [P, GROUP, P], bf16)
        bias3 = sb("bias3", [P, TILES, P], bf16)

        K4, K2 = range(SLOTS), range(2)

        def slots(name, width=P, dt=f32):
            return [sb(f"{name}{k}", [P, GROUP, width], dt) for k in K4]

        X, AT = slots("X"), slots("AT")
        IA = [sb(f"IA{k}", [P, 1 + GROUP, P]) for k in K4]
        A0 = slots("A0")
        AD = slots("AD")
        hT0, gT, x3T = slots("hT0_"), slots("gT"), slots("x3T")
        rT = slots("rT")
        xT = slots("xT", 2 * P)
        z = slots("z")
        t = [slots(f"t{l}_") for l in range(3)]
        xn = [slots(f"x{l + 1}_") for l in range(3)]
        own, xb = slots("own"), slots("xb")
        bdeg, res = slots("bdeg"), slots("res")
        hh = slots("hh", 2 * P)
        isedge = slots("isedge", P, bf16)
        stats, mv = [slots(f"stats{l}_", 6) for l in range(3)], [slots(f"mv{l}_", 2) for l in range(3)]
        std = [[sb(f"std{l}_{k}", [P, GROUP]) for k in K4] for l in range(3)]
        rstd = [[sb(f"rstd{l}_{k}", [P, GROUP]) for k in K4] for l in range(3)]
        shift = [sb(f"shift{k}", [P, GROUP]) for k in K4]
        maskg = [sb(f"maskg{k}", [P, GROUP]) for k in K4]
        sums = sb("sums", [P, SLOTS, 2, GROUP])
        deg = sums[:, :, 0, :]
        rdeg = sb("rdeg", [P, SLOTS, GROUP])
        rs0 = sb("rs0", [P, SLOTS, GROUP])
        rsafe = sb("rsafe", [P, SLOTS, GROUP])
        rsq = sb("rsq", [P, SLOTS, GROUP])
        dis0 = sb("dis0", [P, SLOTS, GROUP])
        dis = sb("dis", [P, SLOTS, GROUP])

        cnt = sb("cnt", [P, B], bf16)
        cntf = sb("cntf", [P, B])
        off = sb("off", [P, B])
        most = sb("most", [1, 1])
        most_i = sb("most_i", [1, 1], i32)

        gA = [sb(f"gA{q}", [P, P]) for q in K2]
        gH = [sb(f"gH{q}", [P, 3, P]) for q in K2]
        gHu = [sb(f"gHu{q}", [P, 2, P], f32r) for q in K2]
        gHl = [sb(f"gHl{q}", [P, 2, P], f32r) for q in K2]
        gAT = [sb(f"gAT{q}", [P, 3, P], bf16) for q in K2]
        rest = sb("rest", [P, P])
        gRES = [sb(f"gRES{q}", [P, P]) for q in K2]
        nz = [sb(f"nz{q}", [P, P]) for q in K2]
        rank = [sb(f"rank{q}", [P, P]) for q in K2]
        pos = [sb(f"pos{q}", [P, P], f32r) for q in K2]
        pos32 = sb("pos32", [P, P])
        begun = [sb(f"begun{q}", [P, CAPACITY], bf16) for q in K2]
        S = [sb(f"S{q}", [P, CAPACITY], f32r) for q in K2]
        T = [sb(f"T{c}", [P, CH], f32r) for c in K2]
        T16 = [sb(f"T16_{c}", [P, CH], bf16) for c in K2]
        hT = [sb(f"hT{c}", [P, CH]) for c in K2]
        ST = [sb(f"ST{c}", [P, TILES, P]) for c in K2]
        sq = [sb(f"sq{c}", [P, TILES, P]) for c in K2]
        WS = [sb(f"WS{c}", [P, TILES, P]) for c in K2]
        yn = [sb(f"yn{c}", [P, TILES, P]) for c in K2]
        ssum = [sb(f"ssum{c}", [P, TILES]) for c in K2]
        esd = [sb(f"esd{c}", [P, TILES]) for c in K2]
        erstd = [sb(f"erstd{c}", [P, TILES]) for c in K2]
        osb = [sb(f"osb{q}", [P, P]) for q in K2]
        gout = [sb(f"gout{q}", [P, P]) for q in K2]
        tout = [sb(f"tout{q}", [P, P]) for q in K2]
        ostats = [sb(f"ostats{q}", [P, 6]) for q in K2]
        omv = [sb(f"omv{q}", [P, 2]) for q in K2]
        ostd = [sb(f"ostd{q}", [P, 1]) for q in K2]
        orstd = [sb(f"orstd{q}", [P, 1]) for q in K2]
        y4 = [sb(f"y4{q}", [P, P]) for q in K2]
        acc = sb("acc", [P, P])
        goff = sb("goff", [P, 1])
        invp = 1.0 / P

        bank = [ctx.enter_context(nc.psum_tensor(f"bank{n}", [P, 512], f32)) for n in range(8)]

        def results(bk, width=P):
            return bk[:, 0:GROUP * width].rearrange("p (g f) -> p g f", g=GROUP)

        u_flat = bank[0][:, 0:GROUP * P]
        hT_ps = u_ps = results(bank[0])
        y_ps = results(bank[1])
        sums_ps = bank[1][:, GROUP * P:GROUP * (P + 2)].rearrange("p (a g) -> p a g", a=2)
        xT_ps = results(bank[2], 2 * P)
        p_ps = results(bank[3])
        q_ps = results(bank[4])
        gT_ps = o_ps = results(bank[5])
        x3T_ps = results(bank[6])
        hh_ps = results(bank[6], 2 * P)
        off_ps, graph_ps = bank[7][:, 0:B], bank[7][:, B:2 * B]

        def flat(ap):
            return ap[:, :, :].rearrange("p g f -> p (g f)")

        V_ps = bank[0][:, 0:CH]
        H_ps = bank[1][:, 0:CH]
        ST_ps = bank[2][:, 0:CH].rearrange("p (t f) -> p t f", t=TILES)
        M_ps = bank[3][:, 0:CH].rearrange("p (t f) -> p t f", t=TILES)
        S_ps = bank[4][:, 0:CH]
        Y_ps = [bank[5 + c][:, 0:CH].rearrange("p (t f) -> p t f", t=TILES) for c in K2]
        O_ps = bank[7][:, 0:P]

        s_const = sem("const_loaded")
        s_mask = sem("mask_loaded")
        s_setp = sem("pool_setup_done")
        s_diff = sem("diagonal_of_diff")
        s_ident = sem("identities_placed")
        s_v = sem("vector_setup_steps")
        s_scaled = sem("scaled_identity_ready")
        s_bias = sem("biases_split")

        x_loaded = [sem(f"x_loaded{k}") for k in K4]
        a_loaded = [sem(f"a_loaded{k}") for k in K4]
        at_loaded = [sem(f"at_loaded{k}") for k in K4]
        names = ["a0_ready", "ai_done", "ad_ready", "sums_ready", "cnt_copied", "rs0_done", "rsafe_ready", "rsq_ready", "dis0_done", "dis_ready",
                 "isedge_ready", "hT_psum", "hT_ready", "u_psum", "rT_ready", "y_psum", "mask_ready",
                 "t0_done", "stats0", "var0", "std0", "rstd0", "x1_ready",
                 "xT_psum", "xT_ready", "p_psum", "p_ready", "q_psum", "z_done",
                 "t1_done", "stats1", "var1", "std1", "rstd1", "x2_ready",
                 "gT_psum", "gT_ready", "o_psum", "xb_ready",
                 "t2_done", "stats2", "var2", "std2", "rstd2", "shift2", "x3_ready",
                 "x3T_psum", "x3T_ready", "hh_psum", "hh_ready", "bdeg_done", "res_ready"]
        s = {n: sem(n) for n in names}
        stored = [sem(f"group_stored{k}") for k in K4]

        cnt_ready = sem("cnt_ready")
        count_psum = sem("count_psum")
        most_done = sem("most_done")
        off_ready = sem("off_ready")
        most_ready = sem("most_ready")

        ga_loaded = [sem(f"ga_loaded{q}") for q in K2]
        gh_loaded = [sem(f"gh_loaded{q}") for q in K2]
        gres_loaded = [sem(f"gres_loaded{q}") for q in K2]
        names3 = ["split_up", "split_done", "at_high", "at_rest", "at_middle", "at_split", "nz_done", "rank_done", "pos_ready", "begun_ready", "O_ready",
                  "gamma_done", "t_done", "stats_done", "var_ready", "ostd_ready", "orstd_done", "out_ready",
                  "shifted", "acc_done"]
        chunk_names = ["S_psum", "S_ready", "V_psum", "T_ready", "T16_ready", "H_psum", "hT_ready", "M_psum", "WS_ready",
                       "ST_psum", "ST_ready", "Y_psum", "sq_ready", "ssum_ready", "sd_ready", "rstd_done",
                       "yn_ready", "O_psum"]
        b = {n: sem("e_" + n) for n in names3}
        e = {n: [sem(f"e_{n}{c}") for c in K2] for n in chunk_names}
        out_stored = [sem(f"out_stored{q}") for q in K2]

        SLOT_STORED = ROUNDS * 2 * 16 + 1

        def staggered(stages, r, counts, ages):
            times = [(at + APART * k, i, k) for i, (at, _) in enumerate(stages) for k in K4]
            for at, i, k in sorted((at % PERIOD, i, k) for at, i, k in times):
                age = int((stages[i][0] + APART * k) // PERIOD)
                assert age < 2
                if age in ages:
                    stages[i][1](k, r - age, counts[age][k])

        def count(r):
            return [SLOTS * r + k + 1 for k in K4]

        def is_last(r):
            return isinstance(r, int) and r == ROUNDS - 1

        def rounds(engine, stages, first=None, last=None, count_first=False):
            staggered(stages, 0, (count(0), None), (0,))
            if first is not None:
                first()
            staggered(stages, 1, (count(1), count(0)), (0, 1))
            with engine.Fori(2, ROUNDS - 1) as r:
                counts = [[engine.snap(n) for n in count(r - age)] for age in range(2)]
                if count_first:
                    for n in counts[1]:
                        engine.wait_ge(s["mask_ready"], n)
                staggered(stages, r, counts, (0, 1))
            if last is not None:
                last()
            staggered(stages, ROUNDS - 1, (count(ROUNDS - 1), count(ROUNDS - 2)), (0, 1))
            staggered(stages, ROUNDS, (None, count(ROUNDS - 1)), (1,))

        def wait_past(engine, semaphore, n):
            if not isinstance(n, int) or n > 0:
                engine.wait_ge(semaphore, n)

        AGES = 3

        def flow(stages, p, counts, ages):
            times = [(at + PERIOD3 / 2 * q, i, q) for i, (at, _) in enumerate(stages) for q in K2]
            for at, i, q in sorted((at % PERIOD3, i, q) for at, i, q in times):
                age = int((stages[i][0] + PERIOD3 / 2 * q) // PERIOD3)
                assert age < AGES
                if age in ages:
                    stages[i][1](q, 2 * (p - age) + q, lambda d=0: counts(q - 2 * age - d))

        def pairs(engine, stages):
            last = B // 2 - 1

            def constant(p):
                return lambda d: 2 * p + 1 + d

            for p in range(AGES):
                flow(stages, p, constant(p), range(p + 1))
            with engine.Fori(AGES, last) as p:
                counts = {d: engine.snap(2 * p + 1 + d) for d in range(-2 * AGES, 2)}
                flow(stages, p, counts.get, range(AGES))
            for late in range(AGES):
                flow(stages, last + late, constant(last + late), range(late, AGES))

        def wait_chunk(engine, semaphores, c, count):
            if c == 0:
                wait_past(engine, semaphores[1], count(1))
            else:
                engine.wait_ge(semaphores[0], count())

        block = ctx.enter_context(nc.Block())

        @block.sync
        def _(sp):
            sp.dma_start(const[:, :], const_d).then_inc(s_const, 16)
            sp.dma_start(mask8[:, :], mask_d).then_inc(s_mask, 16)

            def load(dst, src, group, sm):
                sp.dma_start(dst.rearrange("p g f -> p (g f)"), src[bass.ds(group, 1), :, :].rearrange("o p c -> p (o c)")).then_inc(sm, 16)

            def adj_of(k):
                return IA[k][:, 1:1 + GROUP, :]

            for k in K4:
                load(adj_of(k), a_d, k, a_loaded[k])
                load(X[k][:, :, :], x_d, k, x_loaded[k])
                load(AT[k][:, :, :], at_d, k, at_loaded[k])

            def next_x(k, r, n):
                if not is_last(r):
                    sp.wait_ge(s["t0_done"], n)
                    load(X[k][:, :, :], x_d, SLOTS * (r + 1) + k, x_loaded[k])

            def next_at(k, r, n):
                if not is_last(r):
                    sp.wait_ge(s["y_psum"], n)
                    sp.wait_ge(s["ai_done"], n)
                    load(AT[k][:, :, :], at_d, SLOTS * (r + 1) + k, at_loaded[k])

            def next_a(k, r, n):
                if not is_last(r):
                    sp.wait_ge(s["xT_psum"], n)
                    load(adj_of(k), a_d, SLOTS * (r + 1) + k, a_loaded[k])

            def keep(buf, dst, ready):
                def stage(k, r, n):
                    sp.wait_ge(s[ready], n)
                    sp.dma_start(dst[bass.ds(GROUP * (SLOTS * r + k), GROUP), :, :].rearrange("g p f -> p g f"),
                                 buf[k][:, :, :]).then_inc(stored[k], 16)
                return stage

            def load_a(g, q):
                sp.dma_start(gA[q][:, :], a_g[bass.ds(g, 1), :, :].rearrange("o p c -> p (o c)")).then_inc(ga_loaded[q], 16)

            def load_h(g, q):
                sp.dma_start(gH[q][:, 0:2, :].rearrange("p a c -> p (a c)"),
                             hh_s[bass.ds(g, 1), :, :].rearrange("o p c -> p (o c)")).then_inc(gh_loaded[q], 16)
                sp.dma_start(gH[q][:, 2, :], at_g[bass.ds(g, 1), :, :].rearrange("o p c -> p (o c)")).then_inc(gh_loaded[q], 16)

            def load_res(g, q):
                sp.dma_start(gRES[q][:, :], res_s[bass.ds(g, 1), :, :].rearrange("o p c -> p (o c)")).then_inc(gres_loaded[q], 16)

            def first_graphs():
                sp.wait_ge(stored[0], 33)
                for q in K2:
                    load_a(q, q)
                    load_h(q, q)
                    load_res(q, q)

            rounds(sp, [(3.97, next_at), (5.22, next_x), (11.24, next_a), (29.97, keep(res, res_s, "res_ready")), (31.68, keep(hh, hh_s, "hh_ready"))], last=first_graphs)
            for k in K4:
                sp.wait_ge(stored[k], SLOT_STORED)

            def store(q, g, count):
                sp.wait_ge(b["out_ready"], count())
                sp.dma_start(out_d[bass.ds(g, 1), :, :].rearrange("o p c -> p (o c)"), y4[q][:, :]).then_inc(out_stored[q], 16)

            sp.wait_ge(most_ready, 1)
            fullest = sp.value_load(most_i[0:1, 0:1], min_val=0, max_val=P * P)
            with sp.If(fullest > CAPACITY):
                sp.wait_ge(ga_loaded[0], 16)
                sp.wait_ge(gh_loaded[0], 32)
                sp.wait_ge(gres_loaded[0], 16)
                with sp.Fori(0, B) as g:
                    load_a(g, 0)
                    load_h(g, 0)
                    load_res(g, 0)
                    store(0, g, lambda: g + 1)
                sp.wait_ge(out_stored[0], 16 * B + 1)
            with sp.Else():
                def next_a(q, g, count):
                    if not isinstance(g, int) or g < B - 2:
                        sp.wait_ge(b["nz_done"], count())
                        load_a(g + 2, q)

                def next_h(q, g, count):
                    if not isinstance(g, int) or g < B - 2:
                        sp.wait_ge(b["split_done"], count())
                        sp.wait_ge(b["at_split"], count())
                        load_h(g + 2, q)

                def next_res(q, g, count):
                    if not isinstance(g, int) or g < B - 2:
                        sp.wait_ge(b["t_done"], count())
                        load_res(g + 2, q)

                pairs(sp, [(0.49, next_a), (3.62, next_h), (17.73, next_res), (20.45, store)])
                for q in K2:
                    sp.wait_ge(out_stored[q], 8 * B + 1)

        @block.gpsimd
        def _(pool):
            nc.gpsimd.memset(zeros[:, :], 0.0)
            nc.gpsimd.memset(ident[:, :], 0.0)
            nc.gpsimd.memset(ones_b[:, :], 1.0)
            nc.gpsimd.memset(tri[:, :], 1.0)
            nc.gpsimd.memset(eps_col[:, :], LN_EPS)
            nc.gpsimd.memset(bias0[:, :, :], 0.0)
            nc.gpsimd.memset(bias1[:, :, :], 0.0)
            nc.gpsimd.memset(bias3[:, :, :], 0.0)
            nc.gpsimd.memset(ones_f[:, :], 1.0)
            nc.gpsimd.memset(diff[:, :], 0.0).then_inc(s_setp, 1)
            pool.wait_ge(s_setp, 1)
            nc.gpsimd.affine_select(out=ident[:, :], in_=ident[:, :], compare_op=ALU.not_equal, fill=1.0,
                                    base=0, pattern=[[-1, P]], channel_multiplier=1).then_inc(s_setp, 1)

            def spread_rows(row):
                return row.unsqueeze(1).to_broadcast([P, GROUP, P])

            def spread_cols(ap):
                return ap.unsqueeze(2).to_broadcast([P, GROUP, P])

            def index_constants():
                nc.gpsimd.iota(edge_i[:, :], pattern=[[1, CAPACITY]], base=0, channel_multiplier=0)
                nc.gpsimd.affine_select(out=tri[:, :], in_=tri[:, :], compare_op=ALU.is_ge, fill=0.0,
                                        base=-1, pattern=[[1, P]], channel_multiplier=-1)
                nc.gpsimd.affine_select(out=diff[:, :], in_=diff[:, :], compare_op=ALU.not_equal, fill=1.0,
                                        base=0, pattern=[[-1, P]], channel_multiplier=1).then_inc(s_diff, 1)
                pool.wait_ge(s_diff, 1)
                nc.gpsimd.affine_select(out=diff[:, :], in_=diff[:, :], compare_op=ALU.not_equal, fill=-1.0,
                                        base=-1, pattern=[[-1, P]], channel_multiplier=1).then_inc(s_setp, 1)

            pool.wait_ge(s_scaled, 1)

            def add_scaled(k, r, n):
                pool.wait_ge(a_loaded[k], 16 * r + 16)
                nc.gpsimd.tensor_tensor(A0[k][:, :, :], IA[k][:, 1:1 + GROUP, :], spread_rows(scaled_id[:, :]), ALU.add).then_inc(s["a0_ready"], 1)

            def fix_mask(k, r, n):
                nc.gpsimd.tensor_copy(maskg[k][:, :], mask[:, bass.ds(GROUP * (SLOTS * r + k), GROUP)]).then_inc(s["mask_ready"], 1)

            def add_identity(k, r, n):
                pool.wait_ge(at_loaded[k], 16 * r + 16)
                wait_past(pool, s["gT_psum"], n - SLOTS)
                nc.gpsimd.tensor_tensor(AD[k][:, :, :], AT[k][:, :, :], spread_rows(ident[:, :]), ALU.add).then_inc(s["ai_done"], 1)

            def scale_adj(k, r, n):
                pool.wait_ge(s["ai_done"], n)
                pool.wait_ge(s["dis_ready"], n)
                nc.gpsimd.tensor_tensor(AD[k][:, :, :], AD[k][:, :, :], spread_cols(dis[:, k, :]), ALU.mult).then_inc(s["ad_ready"], 1)

            def beta_degree(k, r, n):
                pool.wait_ge(s["sums_ready"], n)
                wait_past(pool, s["res_ready"], n - SLOTS)
                nc.gpsimd.tensor_tensor(bdeg[k][:, :, :], spread_rows(C["beta"]), spread_cols(deg[:, k, :]), ALU.mult).then_inc(s["bdeg_done"], 1)

            def keep_counts(k, r, n):
                nc.gpsimd.tensor_copy(cntf[:, bass.ds(GROUP * (SLOTS * r + k), GROUP)], sums[:, k, 1, :]).then_inc(s["cnt_copied"], 1)

            def add_bias2(k, r, n):
                pool.wait_ge(s["x2_ready"], n)
                nc.gpsimd.tensor_tensor(xb[k][:, :, :], xn[1][k][:, :, :], spread_rows(C["L2_b"]), ALU.add).then_inc(s["xb_ready"], 1)

            def residual(k, r, n):
                pool.wait_ge(s["x3_ready"], n)
                pool.wait_ge(s["bdeg_done"], n)
                pool.wait_ge(stored[k], 32 * r + 1)
                nc.gpsimd.tensor_tensor(res[k][:, :, :], xn[2][k][:, :, :], bdeg[k][:, :, :], ALU.add).then_inc(s["res_ready"], 1)

            rounds(pool, [(0.00, add_scaled), (0.70, add_identity), (1.40, fix_mask), (7.94, beta_degree), (8.64, keep_counts),
                         (9.50, scale_adj), (21.58, add_bias2), (29.28, residual)], first=index_constants)

            def split_upper(q):
                nc.gpsimd.tensor_tensor(gHu[q][:, :, :], gH[q][:, 0:2, :],
                                        zeros[:, :].unsqueeze(1).to_broadcast([P, 2, P]), ALU.add).then_inc(b["split_up"], 1)

            def split_lower(q, n):
                pool.wait_ge(b["split_up"], n)
                nc.gpsimd.tensor_tensor(gHl[q][:, :, :], gH[q][:, 0:2, :], gHu[q][:, :, :].bitcast(f32),
                                        ALU.subtract).then_inc(b["split_done"], 1)

            def split_adj(q, n):
                adj = gH[q][:, 2, :]
                nc.gpsimd.tensor_tensor(gAT[q][:, 0, :], adj, zeros[:, :], ALU.add).then_inc(b["at_high"], 1)
                pool.wait_ge(b["at_high"], n)
                nc.gpsimd.tensor_tensor(rest[:, :], adj, gAT[q][:, 0, :], ALU.subtract).then_inc(b["at_rest"], 1)
                pool.wait_ge(b["at_rest"], n)
                nc.gpsimd.tensor_tensor(gAT[q][:, 1, :], rest[:, :], zeros[:, :], ALU.add).then_inc(b["at_middle"], 1)
                pool.wait_ge(b["at_middle"], n)
                nc.gpsimd.tensor_tensor(gAT[q][:, 2, :], rest[:, :], gAT[q][:, 1, :], ALU.subtract).then_inc(b["at_split"], 1)

            def times_gamma(q, n):
                pool.wait_ge(b["O_ready"], n)
                nc.gpsimd.tensor_tensor(gout[q][:, :], osb[q][:, :], C["gamma"], ALU.mult).then_inc(b["gamma_done"], 1)

            def add_residual(q, n, loads):
                pool.wait_ge(gres_loaded[q], loads)
                pool.wait_ge(b["gamma_done"], n)
                nc.gpsimd.tensor_tensor(tout[q][:, :], gout[q][:, :], gRES[q][:, :], ALU.add).then_inc(b["t_done"], 1)

            pool.wait_ge(most_ready, 1)
            fullest = pool.value_load(most_i[0:1, 0:1], min_val=0, max_val=P * P)
            with pool.If(fullest > CAPACITY):
                with pool.Fori(0, B) as g:
                    pool.wait_ge(gh_loaded[0], 32 * g + 64)
                    split_upper(0)
                    split_lower(0, g + 1)
                    split_adj(0, g + 1)
                    times_gamma(0, g + 1)
                    add_residual(0, g + 1, 16 * g + 32)
            with pool.Else():
                def upper(q, g, count):
                    pool.wait_ge(gh_loaded[q], (g - q) * 16 + 32)
                    wait_past(pool, e["H_psum"][1], count(2))
                    split_upper(q)

                def lower(q, g, count):
                    split_lower(q, count())

                def adj_parts(q, g, count):
                    pool.wait_ge(gh_loaded[q], (g - q) * 16 + 32)
                    wait_past(pool, e["M_psum"][1], count(2))
                    wait_past(pool, b["at_split"], count(1))
                    split_adj(q, count())

                def gamma(q, g, count):
                    times_gamma(q, count())

                def residual3(q, g, count):
                    wait_past(pool, b["out_ready"], count(2))
                    add_residual(q, count(), (g - q) * 8 + 16)

                pairs(pool, [(0.10, upper), (0.92, lower), (1.62, adj_parts), (16.74, gamma), (17.30, residual3)])

        @block.scalar
        def _(act):
            nc.scalar.preload_act_table(ACT.Sqrt)
            act.wait_ge(s_const, 16)
            act.wait_ge(s_setp, 2)
            for k in K4:
                last = nc.scalar.activation(IA[k][:, 0, :], ident[:, :], ACT.Copy)
            last.then_inc(s_ident, 1)

            def ln_std(layer):
                def stage(k, r, n):
                    act.wait_ge(s[f"var{layer}"], n)
                    nc.scalar.activation(std[layer][k][:, :], mv[layer][k][:, :, 1], ACT.Sqrt, bias=eps_col[:, 0:1]).then_inc(s[f"std{layer}"], 1)
                return stage

            def evict(src, dst, wait, done, func=ACT.Copy, **kw):
                def stage(k, r, n):
                    act.wait_ge(s[wait], n)
                    nc.scalar.activation(dst[k][:, :, :], src, func, **kw).then_inc(s[done], 1)
                return stage

            def root_rowsum(k, r, n):
                act.wait_ge(s["rsafe_ready"], n)
                nc.scalar.activation(rsq[:, k, :], rsafe[:, k, :], ACT.Sqrt).then_inc(s["rsq_ready"], 1)

            def keep_sums(k, r, n):
                act.wait_ge(s["t0_done"], n)
                nc.scalar.activation(sums[:, k, :, :], sums_ps, ACT.Copy).then_inc(s["sums_ready"], 1)

            def apply2(k, r, n):
                act.wait_ge(s["shift2"], n)
                for g in range(GROUP):
                    last = nc.scalar.activation(xn[2][k][:, g, :], t[2][k][:, g, :], ACT.Identity, bias=shift[k][:, g:g + 1],
                                                scale=rstd[2][k][:, g:g + 1])
                last.then_inc(s["x3_ready"], 1)

            def keep_hh(k, r, n):
                act.wait_ge(stored[k], 32 * r + 1)
                act.wait_ge(s["hh_psum"], n)
                nc.scalar.activation(hh[k][:, :, :], hh_ps, ACT.Copy).then_inc(s["hh_ready"], 1)

            keep_hT = evict(hT_ps, hT0, "hT_psum", "hT_ready")
            relu_u = evict(u_ps, rT, "u_psum", "rT_ready", ACT.Relu, bias=C["L0_b1"])
            keep_xT = evict(xT_ps, xT, "xT_psum", "xT_ready")
            keep_p = evict(p_ps, own, "p_psum", "p_ready")
            keep_gT = evict(gT_ps, gT, "gT_psum", "gT_ready")
            keep_x3T = evict(x3T_ps, x3T, "x3T_psum", "x3T_ready")
            rounds(act, [(1.56, keep_hT), (2.84, relu_u), (6.46, keep_sums), (7.70, ln_std(0)), (8.24, root_rowsum),
                         (11.44, keep_xT), (13.34, keep_p), (17.42, ln_std(1)), (20.18, keep_gT), (24.88, ln_std(2)),
                         (27.56, apply2), (29.22, keep_x3T), (31.50, keep_hh)])

            def keep_S(q, c, n):
                act.wait_ge(e["S_psum"][c], n)
                nc.scalar.activation(S[q][:, c * CH:(c + 1) * CH], S_ps, ACT.Copy).then_inc(e["S_ready"][c], 1)

            def relu(c, n):
                act.wait_ge(e["H_psum"][c], n)
                nc.scalar.activation(hT[c][:, :], H_ps, ACT.Relu, bias=C["L3_b1"]).then_inc(e["hT_ready"][c], 1)

            def keep_ST(c, n):
                act.wait_ge(e["ST_psum"][c], n)
                nc.scalar.activation(ST[c][:, :, :], ST_ps, ACT.Copy).then_inc(e["ST_ready"][c], 1)

            def square(c, n):
                act.wait_ge(e["Y_psum"][c], n)
                nc.scalar.activation(sq[c][:, :, :], Y_ps[c], ACT.Square).then_inc(e["sq_ready"][c], 1)

            def spread(c, n):
                act.wait_ge(e["ssum_ready"][c], n)
                nc.scalar.activation(esd[c][:, :], ssum[c][:, :], ACT.Sqrt, bias=eps_col[:, 0:1], scale=invp).then_inc(e["sd_ready"][c], 1)

            def weigh(c, n):
                act.wait_ge(e["rstd_done"][c], n)
                for i in range(TILES):
                    last = nc.scalar.activation(yn[c][:, i, :], Y_ps[c][:, i, :], ACT.Copy, scale=erstd[c][:, i:i + 1])
                last.then_inc(e["yn_ready"][c], 1)

            def keep_sum(q, n):
                act.wait_ge(e["O_psum"][1], n)
                nc.scalar.activation(osb[q][:, :], O_ps, ACT.Copy).then_inc(b["O_ready"], 1)

            def out_std(q, n):
                act.wait_ge(b["var_ready"], n)
                nc.scalar.activation(ostd[q][:, :], omv[q][:, 1:2], ACT.Sqrt, bias=eps_col[:, 0:1]).then_inc(b["ostd_ready"], 1)

            act.wait_ge(most_ready, 1)
            fullest = act.value_load(most_i[0:1, 0:1], min_val=0, max_val=P * P)
            with act.If(fullest > CAPACITY):
                with act.Fori(0, B) as g:
                    with act.Fori(0, ALL_CHUNKS) as c:
                        n = g * ALL_CHUNKS + c + 1
                        keep_S(0, 0, n)
                        keep_ST(0, n)
                        relu(0, n)
                        square(0, n)
                        spread(0, n)
                        weigh(0, n)
                    out_std(0, g + 1)
            with act.Else():
                def starts(c):
                    def stage(q, g, count):
                        wait_past(act, e["H_psum"][c], count(2))
                        keep_S(q, c, count())
                    return stage

                def starts_T(c):
                    def stage(q, g, count):
                        wait_past(act, e["WS_ready"][c], count(1))
                        keep_ST(c, count())
                    return stage

                def hidden(c):
                    def stage(q, g, count):
                        wait_past(act, e["Y_psum"][c], count(1))
                        relu(c, count())
                    return stage

                def squares(c):
                    def stage(q, g, count):
                        wait_past(act, e["ssum_ready"][c], count(1))
                        square(c, count())
                    return stage

                def spreads(c):
                    return lambda q, g, count: spread(c, count())

                def weighs(c):
                    def stage(q, g, count):
                        wait_past(act, e["O_psum"][c], count(1))
                        weigh(c, count())
                    return stage

                def sums3(q, g, count):
                    wait_past(act, b["gamma_done"], count(2))
                    keep_sum(q, count())

                def std3(q, g, count):
                    out_std(q, count())

                pairs(act, [(1.06, starts(0)), (2.14, starts(1)), (2.72, starts_T(0)), (4.54, hidden(0)), (5.36, starts_T(1)),
                         (7.12, squares(0)), (8.00, hidden(1)), (9.08, spreads(0)), (9.76, squares(1)), (10.14, weighs(0)),
                         (11.72, spreads(1)), (12.60, weighs(1)), (15.04, sums3), (18.96, std3)])

        @block.vector
        def _(dve):
            step = [0]

            def then(ins):
                ins.then_inc(s_v, 1)
                step[0] += 1
                dve.wait_ge(s_v, step[0])

            dve.wait_ge(s_setp, 2)
            dve.wait_ge(s_const, 16)
            dve.wait_ge(s_mask, 16)
            nc.vector.tensor_copy(mask[:, :], mask8[:, :])
            then(nc.vector.tensor_scalar(w2mean[:, :], C["L0_eps"], 1.0, None, ALU.add))
            nc.vector.tensor_scalar(scaled_id[:, :], ident[:, :], w2mean[:, 0:1], None, ALU.mult).then_inc(s_scaled, 1)

            def split_bias(row, bias, copies, m):
                then(nc.vector.tensor_copy(part[m][:, :], row))
                then(nc.vector.tensor_tensor(split[0][:, :], row, part[m][:, :], ALU.subtract))
                then(nc.vector.tensor_copy(part[m + 1][:, :], split[0][:, :]))
                then(nc.vector.tensor_tensor(split[1][:, :], split[0][:, :], part[m + 1][:, :], ALU.subtract))
                then(nc.vector.tensor_copy(part[m + 2][:, :], split[1][:, :]))
                for r in range(3):
                    for c in range(copies):
                        last = nc.vector.tensor_copy(bias[32 * r:32 * r + 1, c, 0:P], part[m + r][32 * r:32 * r + 1, :])
                last.then_inc(s_bias, 1)

            split_bias(C["L0_b2"], bias0, GROUP, 0)
            for i, counter in enumerate(stored + out_stored):
                nc.vector.memset(seeds[:, i:i + 1], 0.0).then_inc(counter, 1)

            def layer3_constants():
                dve.wait_ge(s_setp, 3)
                then(nc.vector.tensor_copy(edge[:, :], edge_i[:, :]))
                nc.vector.tensor_scalar(edge1[:, :], edge[:, :], 1.0, None, ALU.add)
                nc.vector.tensor_reduce(b2mean[:, :], C["L3_b2"], AX.X, ALU.add)
                then(nc.vector.tensor_reduce(w2mean[:, :], C["L3_W2"], AX.X, ALU.add))
                nc.vector.tensor_scalar(b2mean[:, :], b2mean[:, :], invp, None, ALU.mult)
                then(nc.vector.tensor_scalar(w2mean[:, :], w2mean[:, :], invp, None, ALU.mult))
                nc.vector.tensor_scalar(b2c[:, :], C["L3_b2"], b2mean[:, 0:1], None, ALU.subtract)
                then(nc.vector.tensor_scalar(w2c[:, :], C["L3_W2"], w2mean[:, 0:1], None, ALU.subtract))
                split_bias(b2c[:, :], bias3, TILES, 3)

            split_bias(C["L1_b"], bias1, GROUP, 6)

            def layer_norm(layer):
                def ln_stats(k, r, n):
                    dve.wait_ge(s[f"t{layer}_done"], n)
                    for g in range(GROUP):
                        last = nc.vector.bn_stats(stats[layer][k][:, g, :], t[layer][k][:, g, :])
                    last.then_inc(s[f"stats{layer}"], 1)

                def ln_var(k, r, n):
                    dve.wait_ge(s_const, 16)
                    dve.wait_ge(s[f"stats{layer}"], n)
                    for g in range(GROUP):
                        last = nc.vector.bn_aggr(mv[layer][k][:, g, :], stats[layer][k][:, g, :])
                    last.then_inc(s[f"var{layer}"], 1)

                def ln_rstd(k, r, n):
                    dve.wait_ge(s[f"std{layer}"], n)
                    nc.vector.reciprocal(rstd[layer][k][:, :], std[layer][k][:, :]).then_inc(s[f"rstd{layer}"], 1)

                def ln_apply(k, r, n):
                    dve.wait_ge(s[f"rstd{layer}"], n)
                    for g in range(GROUP):
                        last = nc.vector.tensor_scalar(xn[layer][k][:, g, :], t[layer][k][:, g, :], mv[layer][k][:, g, 0:1],
                                                       rstd[layer][k][:, g:g + 1], ALU.subtract, ALU.mult)
                    last.then_inc(s[f"x{layer + 1}_ready"], 1)

                return ln_stats, ln_var, ln_rstd, ln_apply

            def mark_edges(k, r, n):
                dve.wait_ge(at_loaded[k], 16 * r + 16)
                nc.vector.tensor_scalar(isedge[k][:, :, :], AT[k][:, :, :], 0.0, None, ALU.not_equal).then_inc(s["isedge_ready"], 1)

            def sum0(k, r, n):
                dve.wait_ge(x_loaded[k], 16 * r + 16)
                dve.wait_ge(s["mask_ready"], n)
                dve.wait_ge(s["y_psum"], n)
                for g in range(GROUP):
                    last = nc.vector.scalar_tensor_tensor(t[0][k][:, g, :], y_ps[:, g, :], maskg[k][:, g:g + 1],
                                                          X[k][:, g, :], ALU.mult, ALU.add)
                last.then_inc(s["t0_done"], 1)

            def degrees(k, r, n):
                dve.wait_ge(s["sums_ready"], n)
                nc.vector.reciprocal(rdeg[:, k, :], deg[:, k, :])
                nc.vector.tensor_scalar(rs0[:, k, :], deg[:, k, :], 1.0, 0.0, ALU.add, ALU.is_equal).then_inc(s["rs0_done"], 1)

            def rowsums(k, r, n):
                dve.wait_ge(s["rs0_done"], n)
                nc.vector.scalar_tensor_tensor(rsafe[:, k, :], deg[:, k, :], 1.0, rs0[:, k, :], ALU.add, ALU.add).then_inc(s["rsafe_ready"], 1)

            def inverse_root(k, r, n):
                dve.wait_ge(s["rsq_ready"], n)
                nc.vector.reciprocal(dis0[:, k, :], rsq[:, k, :]).then_inc(s["dis0_done"], 1)

            def guard_root(k, r, n):
                dve.wait_ge(s["dis0_done"], n)
                nc.vector.scalar_tensor_tensor(dis[:, k, :], rs0[:, k, :], 0.0, dis0[:, k, :], ALU.is_equal, ALU.mult).then_inc(s["dis_ready"], 1)

            def sum1a(k, r, n):
                dve.wait_ge(s["rsafe_ready"], n)
                dve.wait_ge(s["q_psum"], n)
                dve.wait_ge(s["p_ready"], n)
                for g in range(GROUP):
                    last = nc.vector.scalar_tensor_tensor(z[k][:, g, :], q_ps[:, g, :], rdeg[:, k, g:g + 1],
                                                          own[k][:, g, :], ALU.mult, ALU.add)
                last.then_inc(s["z_done"], 1)

            def sum1b(k, r, n):
                dve.wait_ge(s["z_done"], n)
                nc.vector.scalar_tensor_tensor(flat(t[1][k]), flat(z[k]), 0.0, flat(xn[0][k]), ALU.max, ALU.add).then_inc(s["t1_done"], 1)

            def sum2(k, r, n):
                dve.wait_ge(s["o_psum"], n)
                dve.wait_ge(s["xb_ready"], n)
                for g in range(GROUP):
                    last = nc.vector.scalar_tensor_tensor(t[2][k][:, g, :], o_ps[:, g, :], dis[:, k, g:g + 1],
                                                          xb[k][:, g, :], ALU.mult, ALU.add)
                last.then_inc(s["t2_done"], 1)

            stats0, var0, rstd0, apply0 = layer_norm(0)
            stats1, var1, rstd1, apply1 = layer_norm(1)
            stats2, var2, rstd2, _ = layer_norm(2)

            def shift2(k, r, n):
                dve.wait_ge(s["rstd2"], n)
                nc.vector.scalar_tensor_tensor(shift[k][:, :], mv[2][k][:, :, 0], -1.0, rstd[2][k][:, :], ALU.mult, ALU.mult).then_inc(s["shift2"], 1)

            def cast_counts(k, r, n):
                if k == 0 and is_last(r):
                    dve.wait_ge(s["cnt_copied"], GROUPS)
                    nc.vector.tensor_copy(cnt[:, :], cntf[:, :]).then_inc(cnt_ready, 1)

            def fullest_graph(k, r, n):
                if k == 0 and is_last(r):
                    dve.wait_ge(count_psum, 1)
                    nc.vector.tensor_copy(off[:, :], off_ps).then_inc(off_ready, 1)
                    nc.vector.tensor_reduce(most[0:1, :], graph_ps[0:1, :], AX.X, ALU.max).then_inc(most_done, 1)
                    dve.wait_ge(most_done, 1)
                    nc.vector.tensor_copy(most_i[0:1, :], most[0:1, :]).then_inc(most_ready, 1)

            rounds(dve, [(0.00, mark_edges), (4.68, sum0), (6.62, stats0), (7.04, degrees), (7.20, var0),
                         (7.36, rowsums), (8.04, rstd0), (8.30, apply0), (8.82, inverse_root), (9.28, guard_root),
                         (13.84, sum1a), (15.32, sum1b), (15.84, stats1), (16.90, var1), (18.02, rstd1),
                         (18.40, apply1), (22.66, sum2), (23.46, stats2), (24.52, var2), (25.32, rstd2),
                         (27.34, shift2), (28.27, cast_counts), (29.47, fullest_graph)],
                   last=layer3_constants, count_first=True)

            def edges(q, g, loads):
                dve.wait_ge(ga_loaded[q], loads)
                nc.vector.tensor_scalar(nz[q][:, :], gA[q][:, :], 0.0, None, ALU.not_equal).then_inc(b["nz_done"], 1)

            def ranks(q, n):
                dve.wait_ge(b["nz_done"], n)
                nc.vector.tensor_tensor_scan(rank[q][:, :], nz[q][:, :], zeros[:, :], 0.0, ALU.add, ALU.add).then_inc(b["rank_done"], 1)

            def ends(c, e0, n):
                dve.wait_ge(e["V_psum"][c], n)
                nc.vector.tensor_tensor(T[c][:, :], V_ps, edge1[:, e0:e0 + CH], ALU.is_equal).then_inc(e["T_ready"][c], 1)

            def ends_bf16(c, n):
                dve.wait_ge(e["T_ready"][c], n)
                nc.vector.tensor_copy(T16[c][:, :], T[c][:, :].bitcast(f32)).then_inc(e["T16_ready"][c], 1)

            def adj_at_start(c, n):
                dve.wait_ge(e["M_psum"][c], n)
                dve.wait_ge(e["ST_ready"][c], n)
                nc.vector.tensor_tensor(WS[c][:, :, :], M_ps, ST[c][:, :, :], ALU.mult).then_inc(e["WS_ready"][c], 1)

            def sum_squares(c, n):
                dve.wait_ge(e["sq_ready"][c], n)
                nc.vector.tensor_reduce(ssum[c][:, :], sq[c][:, :, :], AX.X, ALU.add).then_inc(e["ssum_ready"][c], 1)

            def invert(c, n):
                dve.wait_ge(e["sd_ready"][c], n)
                nc.vector.reciprocal(erstd[c][:, :], esd[c][:, :]).then_inc(e["rstd_done"][c], 1)

            def norm_stats(q, n):
                dve.wait_ge(b["t_done"], n)
                nc.vector.bn_stats(ostats[q][:, :], tout[q][:, :]).then_inc(b["stats_done"], 1)

            def norm_var(q, n):
                dve.wait_ge(s_const, 16)
                dve.wait_ge(b["stats_done"], n)
                nc.vector.bn_aggr(omv[q][:, :], ostats[q][:, :]).then_inc(b["var_ready"], 1)

            def norm_rstd(q, n):
                dve.wait_ge(b["ostd_ready"], n)
                nc.vector.reciprocal(orstd[q][:, :], ostd[q][:, :]).then_inc(b["orstd_done"], 1)

            def norm_apply(q, n, stores):
                dve.wait_ge(b["orstd_done"], n)
                dve.wait_ge(out_stored[q], stores)
                nc.vector.tensor_scalar(y4[q][:, :], tout[q][:, :], omv[q][:, 0:1], orstd[q][:, 0:1],
                                        ALU.subtract, ALU.mult).then_inc(b["out_ready"], 1)

            dve.wait_ge(most_ready, 1)
            dve.wait_ge(off_ready, 1)
            fullest = dve.value_load(most_i[0:1, 0:1], min_val=0, max_val=P * P)
            with dve.If(fullest > CAPACITY):
                with dve.Fori(0, B) as g:
                    edges(0, g, 16 * g + 32)
                    nc.vector.tensor_copy(goff[:, :], off[:, bass.ds(g, 1)])
                    nc.vector.memset(acc[:, :], 0.0)
                    ranks(0, g + 1)
                    dve.wait_ge(b["rank_done"], g + 1)
                    nc.vector.scalar_tensor_tensor(pos32[:, :], rank[0][:, :], goff[:, 0:1], nz[0][:, :],
                                                   ALU.add, ALU.mult).then_inc(b["shifted"], 1)
                    with dve.Fori(0, ALL_CHUNKS) as c:
                        n = g * ALL_CHUNKS + c + 1
                        dve.wait_ge(b["shifted"], n + g)
                        nc.vector.tensor_copy(pos[0][:, :], pos32[:, :]).then_inc(b["pos_ready"], 1)
                        nc.vector.tensor_scalar(begun[0][:, 0:CH], edge[:, 0:CH], goff[:, 0:1], None, ALU.is_ge).then_inc(b["begun_ready"], 1)
                        ends(0, 0, n)
                        ends_bf16(0, n)
                        adj_at_start(0, n)
                        sum_squares(0, n)
                        invert(0, n)
                        dve.wait_ge(b["begun_ready"], n)
                        nc.vector.tensor_scalar(pos32[:, :], pos32[:, :], float(CH), None, ALU.subtract)
                        nc.vector.tensor_scalar(goff[:, :], goff[:, :], float(CH), None, ALU.subtract).then_inc(b["shifted"], 1)
                        dve.wait_ge(e["O_psum"][0], n)
                        nc.vector.tensor_tensor(acc[:, :], acc[:, :], O_ps, ALU.add).then_inc(b["acc_done"], 1)
                        dve.wait_ge(b["acc_done"], n)
                    nc.vector.tensor_copy(osb[0][:, :], acc[:, :]).then_inc(b["O_ready"], 1)
                    norm_stats(0, g + 1)
                    norm_var(0, g + 1)
                    norm_rstd(0, g + 1)
                    norm_apply(0, g + 1, 16 * g + 1)
            with dve.Else():
                def find_edges(q, g, count):
                    edges(q, g, (g - q) * 8 + 16)

                def rank_edges(q, g, count):
                    ranks(q, count())

                def places(q, g, count):
                    dve.wait_ge(b["rank_done"], count())
                    wait_past(dve, e["V_psum"][1], count(2))
                    nc.vector.scalar_tensor_tensor(pos[q][:, :], rank[q][:, :], off[:, bass.ds(g, 1)], nz[q][:, :],
                                                   ALU.add, ALU.mult).then_inc(b["pos_ready"], 1)

                def begin(q, g, count):
                    wait_past(dve, e["S_psum"][1], count(2))
                    wait_past(dve, e["ST_psum"][1], count(2))
                    nc.vector.tensor_scalar(begun[q][:, :], edge[:, :], off[:, bass.ds(g, 1)], None, ALU.is_ge).then_inc(b["begun_ready"], 1)

                def find_ends(c):
                    def stage(q, g, count):
                        wait_past(dve, e["H_psum"][c], count(1))
                        ends(c, c * CH, count())
                    return stage

                def copy_ends(c):
                    def stage(q, g, count):
                        wait_past(dve, e["M_psum"][c], count(1))
                        ends_bf16(c, count())
                    return stage

                def adj_starts(c):
                    def stage(q, g, count):
                        wait_past(dve, e["O_psum"][c], count(1))
                        adj_at_start(c, count())
                    return stage

                def sums3(c):
                    return lambda q, g, count: sum_squares(c, count())

                def inverts(c):
                    def stage(q, g, count):
                        wait_past(dve, e["yn_ready"][c], count(1))
                        invert(c, count())
                    return stage

                def stats3(q, g, count):
                    norm_stats(q, count())

                def var3(q, g, count):
                    norm_var(q, count())

                def rstd3(q, g, count):
                    norm_rstd(q, count())

                def apply3(q, g, count):
                    norm_apply(q, count(), (g - q) * 8 + 1)

                pairs(dve, [(0.00, begin), (0.34, find_edges), (1.02, rank_edges), (1.40, places), (2.34, find_ends(0)),
                         (2.98, copy_ends(0)), (4.06, find_ends(1)), (5.30, copy_ends(1)), (5.86, adj_starts(0)), (8.24, sums3(0)),
                         (9.42, inverts(0)), (9.84, adj_starts(1)), (11.10, sums3(1)), (12.32, inverts(1)), (18.14, stats3),
                         (18.72, var3), (19.46, rstd3), (20.18, apply3)])

        @block.tensor
        def _(pe):
            pe.wait_ge(s_const, 16)
            pe.wait_ge(s_setp, 2)

            def products(out, lhs, rhs, done, bias=None):
                if bias is not None:
                    nc.tensor.matmul(out, ones_b[:, :], bias[:, :, :], start=True, stop=False)
                for g in range(GROUP):
                    last = nc.tensor.matmul(out[:, g, :], lhs(g), rhs(g), start=bias is None,
                                            stop=bias is None or g == GROUP - 1)
                last.then_inc(s[done], 1)

            l3_w = const[:, P * MATS.index("L3_W1a"):P * (MATS.index("L3_W1a") + 2)]

            def hidden0(k, r, n):
                pe.wait_ge(s["a0_ready"], n)
                pe.wait_ge(x_loaded[k], 16 * r + 16)
                wait_past(pe, s["rT_ready"], n - 1)
                products(hT_ps, lambda g: X[k][:, g, :], lambda g: A0[k][:, g, :], "hT_psum")

            def mlp0a(k, r, n):
                pe.wait_ge(s["hT_ready"], n)
                nc.tensor.matmul(u_flat, C["L0_W1"], flat(hT0[k]), start=True, stop=True).then_inc(s["u_psum"], 1)

            def count_row(k, r, n):
                wait_past(pe, s["sums_ready"], n - 1)
                pe.wait_ge(s["isedge_ready"], n)
                for g in range(GROUP):
                    nc.tensor.matmul(sums_ps[:, 0, g:g + 1], AT[k][:, g, :], ones_f[:, :], start=True, stop=True)
                    nc.tensor.matmul(sums_ps[:, 1, g:g + 1], isedge[k][:, g, :], ones_b[:, 0:1], start=True, stop=True)

            def mlp0b(k, r, n):
                if isinstance(r, int) and r == 0:
                    pe.wait_ge(s_bias, 1)
                pe.wait_ge(s["rT_ready"], n)
                products(y_ps, lambda g: rT[k][:, g, :], lambda g: C["L0_W2"], "y_psum", bias=bias0)

            def turn1(k, r, n):
                if isinstance(r, int) and r == 0:
                    pe.wait_ge(s_ident, 1)
                pe.wait_ge(s["x1_ready"], n)
                wait_past(pe, s["xT_ready"], n - 1)
                products(xT_ps, lambda g: xn[0][k][:, g, :], lambda g: IA[k][:, 0:2 + g:1 + g, :], "xT_psum")

            def project1(k, r, n):
                if isinstance(r, int) and r == 0:
                    pe.wait_ge(s_bias, 2)
                pe.wait_ge(s["xT_ready"], n)
                wait_past(pe, s["p_ready"], n - 1)
                wait_past(pe, s["z_done"], n - 1)
                products(p_ps, lambda g: xT[k][:, g, 0:P], lambda g: C["L1_WaT"], "p_psum", bias=bias1)
                products(q_ps, lambda g: xT[k][:, g, P:2 * P], lambda g: C["L1_WbT"], "q_psum")

            def aggregate2(k, r, n):
                pe.wait_ge(s["ad_ready"], n)
                pe.wait_ge(s["x2_ready"], n)
                wait_past(pe, s["t2_done"], n - 1)
                products(gT_ps, lambda g: xn[1][k][:, g, :], lambda g: AD[k][:, g, :], "gT_psum")

            def project2(k, r, n):
                pe.wait_ge(s["gT_ready"], n)
                products(o_ps, lambda g: gT[k][:, g, :], lambda g: C["L2_W"], "o_psum")

            def turn3(k, r, n):
                pe.wait_ge(s["x3_ready"], n)
                wait_past(pe, s["hh_ready"], n - 1)
                for g in range(GROUP):
                    last = nc.tensor.transpose(x3T_ps[:, g, :], xn[2][k][:, g, :], ident[:, :])
                last.then_inc(s["x3T_psum"], 1)

            def project3(k, r, n):
                pe.wait_ge(s["x3T_ready"], n)
                products(hh_ps, lambda g: x3T[k][:, g, :], lambda g: l3_w, "hh_psum")

            def count_graphs(k, r, n):
                if k == 0 and is_last(r):
                    pe.wait_ge(s_setp, 3)
                    pe.wait_ge(cnt_ready, 1)
                    nc.tensor.matmul(off_ps, tri[:, :], cnt[:, :], start=True, stop=True)
                    nc.tensor.matmul(graph_ps, ones_b[:, :], cnt[:, :], start=True, stop=True).then_inc(count_psum, 1)

            rounds(pe, [(0.90, hidden0), (2.04, mlp0a), (2.48, count_row), (3.42, mlp0b), (10.38, turn1),
                         (12.16, project1), (19.54, aggregate2), (20.80, project2), (28.58, turn3), (28.87, count_graphs),
                         (30.44, project3)])

            pe.wait_ge(s["hh_ready"], GROUPS)
            pe.wait_ge(s_bias, 3)

            def start_rows(q, c, n):
                nc.tensor.matmul(S_ps, diff[:, :], begun[q][:, c * CH:(c + 1) * CH], start=True, stop=True).then_inc(e["S_psum"][c], 1)

            def start_columns(q, c, n):
                for i in range(TILES):
                    e0 = c * CH + i * P
                    last = nc.tensor.matmul(ST_ps[:, i, :], begun[q][:, e0:e0 + P], diff[:, :], start=True, stop=True)
                last.then_inc(e["ST_psum"][c], 1)

            def place(q, c, n):
                pe.wait_ge(e["S_ready"][c], n)
                nc.tensor.matmul(V_ps, pos[q][:, :], S[q][:, c * CH:(c + 1) * CH], start=True, stop=True).then_inc(e["V_psum"][c], 1)

            def gather(q, c, n):
                for i, half in enumerate((gHu, gHl)):
                    nc.tensor.matmul(H_ps, half[q][:, 0, :], S[q][:, c * CH:(c + 1) * CH], start=i == 0, stop=False)
                pe.wait_ge(e["T_ready"][c], n)
                for i, half in enumerate((gHu, gHl)):
                    last = nc.tensor.matmul(H_ps, half[q][:, 1, :], T[c][:, :], start=False, stop=i == 1)
                last.then_inc(e["H_psum"][c], 1)

            def rows(q, c):
                for i in range(TILES):
                    for m in range(3):
                        last = nc.tensor.matmul(M_ps[:, i, :], T16[c][:, i * P:(i + 1) * P], gAT[q][:, m, :],
                                                start=m == 0, stop=m == 2)
                last.then_inc(e["M_psum"][c], 1)

            def mlp(c, n):
                pe.wait_ge(e["hT_ready"][c], n)
                nc.tensor.matmul(Y_ps[c].rearrange("p t f -> p (t f)"), ones_b[:, :], flat(bias3), start=True, stop=False)
                for i in range(TILES):
                    last = nc.tensor.matmul(Y_ps[c][:, i, :], hT[c][:, i * P:(i + 1) * P], w2c[:, :], start=False, stop=i == TILES - 1)
                last.then_inc(e["Y_psum"][c], 1)

            def scatter(c, n, start, stop):
                pe.wait_ge(e["yn_ready"][c], n)
                pe.wait_ge(e["WS_ready"][c], n)
                for i in range(TILES):
                    last = nc.tensor.matmul(O_ps, WS[c][:, i, :], yn[c][:, i, :],
                                            start=start and i == 0, stop=stop and i == TILES - 1)
                last.then_inc(e["O_psum"][c], 1)

            pe.wait_ge(most_ready, 1)
            fullest = pe.value_load(most_i[0:1, 0:1], min_val=0, max_val=P * P)
            with pe.If(fullest > CAPACITY):
                with pe.Fori(0, B) as g:
                    with pe.Fori(0, ALL_CHUNKS) as c:
                        n = g * ALL_CHUNKS + c + 1
                        pe.wait_ge(b["begun_ready"], n)
                        start_rows(0, 0, n)
                        start_columns(0, 0, n)
                        pe.wait_ge(b["pos_ready"], n)
                        place(0, 0, n)
                        pe.wait_ge(b["split_done"], g + 1)
                        gather(0, 0, n)
                        pe.wait_ge(b["at_split"], g + 1)
                        pe.wait_ge(e["T16_ready"][0], n)
                        rows(0, 0)
                        mlp(0, n)
                        scatter(0, n, True, True)
            with pe.Else():
                def rows3(c):
                    def stage(q, g, count):
                        pe.wait_ge(b["begun_ready"], count())
                        wait_chunk(pe, e["S_ready"], c, count)
                        start_rows(q, c, count())
                    return stage

                def columns3(c):
                    def stage(q, g, count):
                        pe.wait_ge(b["begun_ready"], count())
                        wait_chunk(pe, e["ST_ready"], c, count)
                        start_columns(q, c, count())
                    return stage

                def places3(c):
                    def stage(q, g, count):
                        pe.wait_ge(b["pos_ready"], count())
                        wait_chunk(pe, e["T_ready"], c, count)
                        place(q, c, count())
                    return stage

                def gather3(c):
                    def stage(q, g, count):
                        pe.wait_ge(b["split_done"], count())
                        wait_chunk(pe, e["hT_ready"], c, count)
                        gather(q, c, count())
                    return stage

                def adj_rows(c):
                    def stage(q, g, count):
                        pe.wait_ge(b["at_split"], count())
                        wait_chunk(pe, e["WS_ready"], c, count)
                        pe.wait_ge(e["T16_ready"][c], count())
                        rows(q, c)
                    return stage

                def mlp3(c):
                    def stage(q, g, count):
                        wait_past(pe, e["yn_ready"][c], count(1))
                        mlp(c, count())
                    return stage

                def scatter3(c):
                    def stage(q, g, count):
                        if c == 0:
                            wait_past(pe, b["O_ready"], count(1))
                        scatter(c, count(), c == 0, c == 1)
                    return stage

                pairs(pe, [(0.62, rows3(0)), (0.80, columns3(0)), (1.76, rows3(1)), (1.96, places3(0)), (3.02, gather3(0)),
                         (3.68, places3(1)), (3.86, columns3(1)), (4.04, adj_rows(0)), (5.22, mlp3(0)), (6.04, gather3(1)),
                         (6.70, adj_rows(1)), (8.70, mlp3(1)), (11.10, scatter3(0)), (14.10, scatter3(1))])


def kernel(x, adj, nodemask, L0_gnn_W1, L0_gnn_b1, L0_gnn_W2, L0_gnn_b2, L0_gnn_eps, L1_gnn_W, L1_gnn_b,
           L2_gnn_weight, L2_gnn_bias, L3_gnn_W1, L3_gnn_b1, L3_gnn_W2, L3_gnn_b2, L3_gnn_gamma, L3_gnn_beta):
    import numpy as np
    import concourse.bacc as bacc
    from concourse.bass_utils import run_bass_kernel_spmd

    x, adj = np.asarray(x), np.asarray(adj)

    def grouped(a):
        return np.ascontiguousarray(a.reshape(GROUPS, GROUP, P, P).transpose(0, 2, 1, 3).reshape(GROUPS, P, GW))

    adj_t = np.ascontiguousarray(adj.transpose(0, 2, 1))
    w1 = np.asarray(L1_gnn_W)
    w3 = np.asarray(L3_gnn_W1)
    mats = [L0_gnn_W1, L0_gnn_W2, w1[:, :P].T, w1[:, P:].T, L2_gnn_weight, w3[:P], w3[P:], L3_gnn_W2]
    rows = [L0_gnn_b2, L1_gnn_b, L2_gnn_bias, L3_gnn_b2, L3_gnn_gamma, L3_gnn_beta]
    cols = [np.asarray(L0_gnn_b1).reshape(P, 1), np.broadcast_to(np.asarray(L0_gnn_eps).reshape(1, 1), (P, 1)),
            np.asarray(L3_gnn_b1).reshape(P, 1)]
    consts = np.ascontiguousarray(np.concatenate(
        [np.asarray(m) for m in mats] + [np.broadcast_to(np.asarray(r).reshape(1, P), (P, P)) for r in rows] + cols, axis=1))
    arrays = {
        "x_groups": grouped(x), "adj_groups": grouped(adj), "adjT_groups": grouped(adj_t),
        "nodemask_T": np.ascontiguousarray(np.asarray(nodemask).T).view(np.uint8), "constants": consts,
        "adj": np.ascontiguousarray(adj), "adj_T": adj_t,
    }
    nc = bacc.Bacc("TRN2", target_bir_lowering=False, num_devices=1)
    ap = {n: nc.dram_tensor(n, a.shape, mybir.dt.from_np(a.dtype), kind="ExternalInput").ap() for n, a in arrays.items()}
    out = nc.dram_tensor("out", (B, P, P), mybir.dt.float32, kind="ExternalOutput").ap()
    gnn_stack(nc, ap["x_groups"], ap["adj_groups"], ap["adjT_groups"], ap["nodemask_T"], ap["constants"],
              ap["adj"], ap["adj_T"], out)
    r = run_bass_kernel_spmd(nc, [arrays], core_ids=[0])
    return r.results[0]["out"]
```
